# Optimizing a Trainium2 kernel written in Bass

```python
import numpy as np
import jax
import jax.numpy as jnp

def _softmax(x, axis=-1):
    return jax.nn.softmax(x, axis=axis)
def _gelu(x):
    return jax.nn.gelu(x, approximate=True)
def _silu(x):
    return jax.nn.silu(x)
def _sigmoid(x):
    return jax.nn.sigmoid(x)
def _layernorm(x, axis=-1, eps=1e-5):
    m = jnp.mean(x, axis=axis, keepdims=True)
    v = jnp.var(x, axis=axis, keepdims=True)
    return (x - m) / jnp.sqrt(v + eps)
def _scatter_add(tgt, idx, src, axis=0):
    return tgt.at[idx].add(src)
def _segment_sum(src, seg, n):
    return jax.ops.segment_sum(src, seg, n)

kernel_name = 'mk_conv_preact_d2_conv_nchw256_b1e158'

def setup_inputs(seed: int = 0):
    np.random.seed(seed)
    _w = jnp.asarray
    def _rec_inputs():
        import jax
        import jax.numpy as jnp
        _gk = jax.random.key(seed)
        x = -0.000125 + 0.9999 * jax.random.normal(jax.random.fold_in(_gk, 1), (8, 256, 128, 128), jnp.float32)
        return x
    x = _rec_inputs()
    def _L0_conv_setup():
        import jax, jax.numpy as jnp
        import numpy as np
        HEADS = 4
        DIM_HEAD = 32
        EPS = 1e-05
        key = jax.random.key(seed)
        ks = jax.random.split(key, 4)
        B, dim, H, W = (8, 256, 128, 128)
        hidden = HEADS * DIM_HEAD
        x = jax.random.normal(ks[0], (B, dim, H, W), dtype=jnp.float32)
        qkv_w = jax.random.normal(ks[1], (3 * hidden, dim), dtype=jnp.float32) * (1.0 / np.sqrt(dim))
        conv_w = jax.random.normal(ks[2], (dim, hidden), dtype=jnp.float32) * (1.0 / np.sqrt(hidden))
        conv_b = jax.random.normal(ks[3], (dim,), dtype=jnp.float32) * 0.01
        gamma = jnp.ones((dim,), dtype=jnp.float32)
        beta = jnp.zeros((dim,), dtype=jnp.float32)
        return {'x': x, 'qkv_w': qkv_w, 'conv_w': conv_w, 'conv_b': conv_b, 'gamma': gamma, 'beta': beta}
    _L0_conv_all = _L0_conv_setup()
    _L0_conv_in = {k: v for k, v in _L0_conv_all.items() if k in ('qkv_w', 'conv_w', 'conv_b', 'gamma', 'beta', )}
    del _L0_conv_all

    def _L1_conv_setup():
        import jax, jax.numpy as jnp
        import numpy as np
        key = jax.random.key(seed)
        k1, k2, k3, k4 = jax.random.split(key, 4)
        B, C, O, H, W = (32, 256, 256, 56, 56)
        HID = max(C // 16, 8)
        x = jax.random.normal(k1, (B, C, H, W), dtype=jnp.float32)
        w_conv = jax.random.normal(k2, (O, C, 1, 1), dtype=jnp.float32) / np.sqrt(C)
        w_se1 = jax.random.normal(k3, (HID, C), dtype=jnp.float32) / np.sqrt(C)
        w_se_out = jax.random.normal(k4, (O * C, HID), dtype=jnp.float32) / np.sqrt(HID)
        return {'x': x, 'w_conv': w_conv, 'w_se1': w_se1, 'w_se_out': w_se_out}
    _L1_conv_all = _L1_conv_setup()
    _L1_conv_in = {k: v for k, v in _L1_conv_all.items() if k in ('w_conv', 'w_se1', 'w_se_out', )}
    del _L1_conv_all

    return {
        "x": x,
        "L0_conv_qkv_w": _L0_conv_in["qkv_w"],
        "L0_conv_conv_w": _L0_conv_in["conv_w"],
        "L0_conv_conv_b": _L0_conv_in["conv_b"],
        "L0_conv_gamma": _L0_conv_in["gamma"],
        "L0_conv_beta": _L0_conv_in["beta"],
        "L1_conv_w_conv": _L1_conv_in["w_conv"],
        "L1_conv_w_se1": _L1_conv_in["w_se1"],
        "L1_conv_w_se_out": _L1_conv_in["w_se_out"],
    }

def reference(x, L0_conv_qkv_w, L0_conv_conv_w, L0_conv_conv_b, L0_conv_gamma, L0_conv_beta, L1_conv_w_conv, L1_conv_w_se1, L1_conv_w_se_out):
    import jax
    import jax.numpy as jnp
    def _L0_conv_ref(x, qkv_w, conv_w, conv_b, gamma, beta):
        import jax, jax.numpy as jnp
        import numpy as np
        HEADS = 4
        DIM_HEAD = 32
        EPS = 1e-05
        B, C, H, W = x.shape
        N = H * W
        scale = DIM_HEAD ** (-0.5)
        qkv = jnp.einsum('oc,bchw->bohw', qkv_w, x).reshape(B, 3, HEADS, DIM_HEAD, N)
        q, k, v = (qkv[:, 0], qkv[:, 1], qkv[:, 2])
        q = jax.nn.softmax(q, axis=-2) * scale
        k = jax.nn.softmax(k, axis=-1)
        v = v / N
        context = jnp.einsum('bhdn,bhen->bhde', k, v)
        out = jnp.einsum('bhde,bhen->bhdn', context, q)
        out = out.reshape(B, HEADS * DIM_HEAD, H, W)
        y = jnp.einsum('oc,bchw->bohw', conv_w, out) + conv_b[None, :, None, None]
        mean = jnp.mean(y, axis=(2, 3), keepdims=True)
        var = jnp.var(y, axis=(2, 3), keepdims=True)
        y = (y - mean) * jax.lax.rsqrt(var + EPS)
        return y * gamma[None, :, None, None] + beta[None, :, None, None]

    def _L1_conv_ref(x, w_conv, w_se1, w_se_out):
        import jax, jax.numpy as jnp
        import numpy as np
        B, C, H, W = x.shape
        O = w_conv.shape[0]
        pooled = jnp.mean(x, axis=(2, 3))
        hid = jax.nn.silu(pooled @ w_se1.T)
        adapt = (hid @ w_se_out.T).reshape(B, O, C)
        w_b = w_conv[None, :, :, 0, 0] + adapt
        out = jnp.einsum('bihw,boi->bohw', x, w_b)
        return out

    def _gn(v, G=32, eps=1e-5):
        B_, C_, H_, W_ = v.shape
        g = v.reshape(B_, G, C_ // G, H_, W_)
        m = jnp.mean(g, axis=(2, 3, 4), keepdims=True)
        s = jnp.var(g, axis=(2, 3, 4), keepdims=True)
        return ((g - m) / jnp.sqrt(s + eps)).reshape(v.shape)

    def _ln_c(v, eps=1e-6):
        m = jnp.mean(v, axis=1, keepdims=True)
        s = jnp.var(v, axis=1, keepdims=True)
        return (v - m) / jnp.sqrt(s + eps)

    def _ln_t(v, eps=1e-5):
        m = jnp.mean(v, axis=-1, keepdims=True)
        s = jnp.var(v, axis=-1, keepdims=True)
        return (v - m) / jnp.sqrt(s + eps)

    def _to_tokens(v):
        B_, C_, H_, W_ = v.shape
        return v.reshape(B_, C_, H_ * W_).transpose(0, 2, 1)
    def _from_tokens(t, like):
        B_, C_, H_, W_ = like.shape
        return t.transpose(0, 2, 1).reshape(B_, C_, H_, W_)

    x = x + _L0_conv_ref(_gn(x), L0_conv_qkv_w, L0_conv_conv_w, L0_conv_conv_b, L0_conv_gamma, L0_conv_beta)
    x = x + _L1_conv_ref(_gn(x), L1_conv_w_conv, L1_conv_w_se1, L1_conv_w_se_out)
    return x


_drawn_inputs = setup_inputs


def setup_inputs(seed=0):
    import zlib

    import numpy as np

    out = dict(_drawn_inputs(seed))
    spreads = {'L0_conv_gamma': (1.0, 0.6), 'L0_conv_beta': (0.0, 0.1)}
    factors = {'L0_conv_qkv_w': 8.0, 'L0_conv_conv_w': 8.0, 'L0_conv_conv_b': 8.0}
    for name, (base, spread) in spreads.items():
        noise = np.random.default_rng([zlib.crc32(name.encode()), seed]).standard_normal(out[name].shape)
        drawn = base * np.exp(spread * noise) if base else spread * noise
        out[name] = jnp.asarray(drawn.astype(out[name].dtype))
    for name, factor in factors.items():
        out[name] = (out[name] * factor).astype(out[name].dtype)
    return out
```

```python
import concourse.bass as bass
from concourse import mybir
from contextlib import ExitStack

F32 = mybir.dt.float32
ALU = mybir.AluOpType
ACT = mybir.ActivationFunctionType
AXX = mybir.AxisListType.X

P = 128
HEADS, DH = 4, 32
HID = HEADS * DH
GC = 8
T = 512
NT = T // P
EPS = 1e-5
BIG = 3.0e38


def block_program(nc, x, qkv_w, conv_w, conv_b, gamma, beta, w_conv, w_se1, w_se_out, out):
    B, C, H, W = x.shape
    N = H * W
    NH = C // P
    NCH = N // T
    NPR = NCH // 2
    NQ = NPR // 4
    J = w_se1.shape[0]
    G1 = HID + 1

    x_v = x.rearrange("b (h p) r w -> b p h (r w)", p=P)
    out_v = out.rearrange("b (h p) r w -> b p h (r w)", p=P)
    q_dram = nc.dram_tensor("q_dram", (B, P, N), F32, kind="Internal").ap()

    ctx = ExitStack()
    with ctx:
        def sb(name, shape):
            return ctx.enter_context(nc.sbuf_tensor(name, shape, F32))

        def sem(name):
            return ctx.enter_context(nc.semaphore(name))

        x_sb = sb("x_sb", [P, NH, N])
        ident = sb("ident", [P, P])
        ones = sb("ones", [P, P])
        group = sb("group", [P, P])
        headmask = sb("headmask", [P, P])
        powers = sb("powers", [P, NH])
        wqvk = sb("wqvk", [P, NH, 3 * HID])
        convT = sb("convT", [P, C])
        w1T = sb("w1T", [P, NH, C])
        se1T = sb("se1T", [P, NH, J])
        se_out = sb("se_out", [P, NH, C, J])
        vecs = sb("vecs", [P, 3, NH])
        xn = sb("xn", [P, 2, NH, T])
        e_k = sb("e_k", [P, 2, T])
        e_kT = sb("e_kT", [P, NT, P])
        v_sb = sb("v_sb", [P, 2, NT, G1])
        q_sb = sb("q_sb", [P, 2, NT * HEADS, DH])
        qn = sb("qn", [P, 2, NT, G1])
        qT = sb("qT", [P, 2, T])
        qm = sb("qm", [P, NT * HEADS])
        qsum = sb("qsum", [P, NT * HEADS])
        qinv = sb("qinv", [P, 2, NT * HEADS])
        negk = sb("negk", [P, 1])
        negmax = sb("negmax", [P, 2])
        alpha = sb("alpha", [P, 2])
        acc = sb("acc", [P, G1])
        gram = sb("gram", [P, G1])
        bn = sb("bn", [P, NH, NCH, 6])
        mv = sb("mv", [P, NH, 2])
        sm = sb("sm", [P, 24, NH])
        MT = sb("MT", [P, C])
        ctxm = sb("ctxm", [P, P])
        gs = sb("gs", [P, G1])
        pz = sb("pz", [P, C])
        hid = sb("hid", [P, 4, J])
        sq = sb("sq", [P, NH, NCH])
        WB = sb("WB", [P, NH, C])
        (DEV, SVAR, RR, NB, DELTA, D2, VB, RS, A, TT, CC, SQS, AD, MEAN1, VAR1, DEV1, S1, R1, POOL,
         VEC, DD) = (sm[:, n, :] for n in range(21))
        raw = xn[:, :, :, :].rearrange("p a b c -> p (a b c)")
        wq_raw = raw[:, 0:3 * C].rearrange("p (t c) -> p t c", t=3)
        cw_raw = raw[:, 3 * C:4 * C].rearrange("p (t c) -> p t c", t=NH)
        w1_raw = raw[:, 4 * C:6 * C].rearrange("p (t c) -> p t c", t=NH)
        ql = xn[:, :, :, :].rearrange("p a b c -> p a (b c)")
        junk = e_k
        WS = e_kT[:, :, :].rearrange("p t c -> p (t c)").rearrange("p (h o) -> p h o", h=NH)
        pooled = qT[:, 0, 0:NH * P].rearrange("p (h c) -> p h c", h=NH)

        PS = ctx.enter_context(nc.psum_tensor("PS", [P, 8, T], F32))
        ps_k = PS[:, 0, :]
        ps_qv = [PS[:, 1 + 2 * u:3 + 2 * u, :].rearrange("p a (b c) -> p (a b) c", c=2 * HID)
                 for u in range(2)]
        ps_eT, ps_qT, ps_cg = PS[:, 5, :], PS[:, 6, :], PS[:, 7, :]
        ring = [PS[:, 1 + n, :] for n in range(4)]

        w_in = [sem(f"w_in{n}") for n in range(4)]
        se_in = sem("se_in")
        pool_step, consts = sem("pool_step"), sem("consts")
        w_tr, w_cp = sem("w_tr"), sem("w_cp")
        x_in = [sem(f"x_in{n}") for n in range(4)]
        out_st = [sem(f"out_st{n}") for n in range(4)]
        q_st = [sem(f"q_st{n}") for n in range(2)]
        q_in = [sem(f"q_in{n}") for n in range(2)]
        xn_ready, k_ready, qv_ready = sem("xn_ready"), sem("k_ready"), sem("qv_ready")
        negmax_ready, ek_ready, alpha_ready = sem("negmax_ready"), sem("ek_ready"), sem("alpha_ready")
        q_shift, q_exp, q_inv, qn_ready = sem("q_shift"), sem("q_exp"), sem("q_inv"), sem("qn_ready")
        v_ready, eT_ps, eT_sb = sem("v_ready"), sem("eT_ps"), sem("eT_sb")
        qT_ps, qT_sb, cg_ready, cg_used = sem("qT_ps"), sem("qT_sb"), sem("cg_ready"), sem("cg_used")
        ring_full, ring_used, sq_done = sem("ring_full"), sem("ring_used"), sem("sq_done")
        s0 = [sem(f"s0_{n}") for n in range(6)]
        s1 = [sem(f"s1_{n}") for n in range(8)]
        s2 = [sem(f"s2_{n}") for n in range(12)]

        block = ctx.enter_context(nc.Block())
        RING = 2 * 2 * NCH

        @block.sync
        def _(sp):
            sp.dma_start(wq_raw, qkv_w.rearrange("(t p) c -> p t c", p=P)).then_inc(w_in[0], 16)
            sp.dma_start(cw_raw, conv_w.rearrange("(t p) c -> p t c", p=P)).then_inc(w_in[1], 16)
            sp.dma_start(w1_raw, w_conv.rearrange("(t p) c i j -> p t (c i j)", p=P)).then_inc(w_in[2], 16)
            with nc.allow_non_contiguous_dma("vectors and the squeeze weights, once"):
                for n, v in enumerate((conv_b, gamma, beta)):
                    sp.dma_start(vecs[:, n, :], v.rearrange("(h p) -> p h", p=P)).then_inc(w_in[3], 16)
                    sp.wait_ge(w_in[3], 16 * (n + 1))
                for h in range(NH):
                    sp.dma_start(se1T[:, h, :], w_se1[:, h * P:(h + 1) * P].rearrange("j p -> p j")).then_inc(w_in[3], 16)
                    sp.wait_ge(w_in[3], 16 * (h + 4))
                for h in range(NH):
                    sp.dma_start(se_out[:, h, :, :], w_se_out.rearrange("(o h p) j -> h p o j", h=NH, p=P)[h])\
                      .then_inc(se_in, 16)
                    sp.wait_ge(se_in, 16 * (h + 1))
            with sp.Fori(0, B) as b:
                with sp.Fori(0, NPR) as i:
                    for u in range(2):
                        sp.wait_ge(qT_sb, b * NCH + i * 2 + u + 1)
                        sp.dma_start(q_dram[b, :, bass.ds(i * (2 * T) + u * T, T)], qT[:, u, :]).then_inc(q_st[u], 16)
                with sp.Fori(0, NPR // 2) as i:
                    for u in range(2):
                        if u == 0:
                            for v in range(2):
                                sp.wait_ge(q_st[v], (b + 1) * (NPR * 16))
                            sp.wait_ge(qv_ready, (b + 1) * NCH + 1)
                        sp.wait_ge(ring_full, b * RING + i * 8 + u * 4)
                        sp.dma_start(ql[:, u, :], q_dram[b, :, bass.ds(i * (4 * T) + u * (2 * T), 2 * T)])\
                          .then_inc(q_in[u], 16)
                with sp.Fori(0, NQ) as i:
                    for u in range(4):
                        sp.wait_ge(ring_used, b * RING + i * 16 + (2 * NCH + 4 * (u + 1)) + 3)
                        sp.wait_ge(out_st[u], b * (NQ * 16) + i * 16)
                        sp.dma_start(out_v[b, :, :, bass.ds(i * (8 * T) + u * (2 * T), 2 * T)],
                                     x_sb[:, :, bass.ds(i * (8 * T) + u * (2 * T), 2 * T)]).then_inc(out_st[u], 16)
            for u in range(4):
                sp.wait_ge(out_st[u], B * NQ * 16)

        @block.gpsimd
        def _(pool):
            steps = [0]

            def step(ins):
                steps[0] += 1
                ins.then_inc(pool_step, 1)
                pool.wait_ge(pool_step, steps[0])

            step(nc.gpsimd.memset(ident[:, :], 0.0))
            step(nc.gpsimd.affine_select(out=ident[:, :], in_=ident[:, :], compare_op=ALU.not_equal, fill=1.0,
                                         base=0, pattern=[[-1, P]], channel_multiplier=1))
            step(nc.gpsimd.memset(ones[:, :], 1.0))
            step(nc.gpsimd.memset(powers[:, :], -0.5))
            step(nc.gpsimd.memset(v_sb[:, :, :, HID:G1], 1.0))
            step(nc.gpsimd.memset(qn[:, :, :, HID:G1], 1.0))
            for tile, size, value in ((group, GC, 1.0 / GC), (headmask, DH, float(DH) ** -0.5 / N)):
                step(nc.gpsimd.memset(tile[:, :], value))
                v = tile[:, :].rearrange("p (g s) -> p g s", s=size)
                step(nc.gpsimd.affine_select(out=v, in_=v, compare_op=ALU.is_ge, fill=0.0, base=0,
                                             pattern=[[-size, P // size], [0, size]], channel_multiplier=1))
                step(nc.gpsimd.affine_select(out=v, in_=v, compare_op=ALU.is_ge, fill=0.0, base=size - 1,
                                             pattern=[[size, P // size], [0, size]], channel_multiplier=-1))
            pool.sem_inc(consts, 1)

            with pool.Fori(0, B) as b:
                pool.wait_ge(s0[4], b + 1)
                nc.gpsimd.tensor_tensor(RR, S1, powers[:, :], ALU.pow).then_inc(s0[5], 1)
                with pool.Fori(0, NPR) as i:
                    for u in range(2):
                        g = b * NCH + i * 2 + u
                        pool.wait_ge(q_inv, g + 1)
                        pool.wait_ge(cg_ready, g)
                        nc.gpsimd.tensor_tensor(
                            qn[:, u, :, 0:HID].rearrange("p t (e d) -> p t e d", d=DH),
                            q_sb[:, u, :, :].rearrange("p (t e) d -> p t e d", e=HEADS),
                            qinv[:, u, :].rearrange("p (t e) -> p t e", e=HEADS)[:, :, :, None]
                            .to_broadcast([P, NT, HEADS, DH]), ALU.mult).then_inc(qn_ready, 1)
                pool.wait_ge(s1[6], b + 1)
                nc.gpsimd.tensor_tensor(RS, VB, powers[:, :], ALU.pow).then_inc(s1[7], 1)
                pool.wait_ge(s2[4], b + 1)
                nc.gpsimd.tensor_tensor(R1, S1, powers[:, :], ALU.pow).then_inc(s2[5], 1)

        @block.scalar
        def _(act):
            def load_pair(b, i, u):
                act.dma_start(x_sb[:, :, bass.ds(i * (8 * T) + u * (2 * T), 2 * T)],
                              x_v[b, :, :, bass.ds(i * (8 * T) + u * (2 * T), 2 * T)]).then_inc(x_in[u], 16)

            with act.Fori(0, NQ) as i:
                for u in range(4):
                    act.wait_ge(x_in[u], i * 16)
                    load_pair(0, i, u)

            def exp_k(b, g, u):
                act.wait_ge(negmax_ready, g + 1)
                act.wait_ge(eT_ps, g)
                nc.scalar.activation(e_k[:, u, :], ps_k, ACT.Exp, bias=negmax[:, u:u + 1]).then_inc(ek_ready, 1)
                act.wait_ge(cg_used, g)
                nc.scalar.activation(alpha[:, u:u + 1], negmax[:, 1 - u:2 - u], ACT.Exp, scale=-1.0,
                                     bias=negmax[:, u:u + 1]).then_inc(alpha_ready, 1)

            def copy_v(g, u):
                act.wait_ge(q_shift, g + 2)
                act.wait_ge(cg_ready, g)
                nc.scalar.activation(v_sb[:, u, :, 0:HID], ps_qv[u][:, :, HID:2 * HID], ACT.Copy).then_inc(v_ready, 1)

            def exp_q(g, u):
                act.wait_ge(q_shift, g + 2)
                nc.scalar.activation(q_sb[:, u, :, :], q_sb[:, u, :, :], ACT.Exp).then_inc(q_exp, 1)

            def copy_eT(g, u):
                act.wait_ge(eT_ps, g + 2)
                act.wait_ge(cg_ready, g + 1)
                nc.scalar.activation(e_kT[:, :, :], ps_eT.rearrange("p (t c) -> p t c", t=NT), ACT.Copy)\
                  .then_inc(eT_sb, 1)

            def copy_qT(g, u, spilled):
                act.wait_ge(qT_ps, g + 1)
                act.wait_ge(q_st[u], spilled)
                nc.scalar.activation(qT[:, u, :], ps_qT, ACT.Copy).then_inc(qT_sb, 1)

            def image(b, last):
                c0 = b * NCH
                exp_k(b, c0, 0)
                copy_v(c0, 0)
                exp_q(c0, 0)

                def step(i, u):
                    g = c0 + i * 2 + u
                    before = c0 + i * 2 + (u - 1) if u else c0 + (i - 1) * 2 + 1
                    exp_k(b, g, u)
                    copy_eT(before, 1 - u)
                    copy_v(g, u)
                    copy_qT(before, 1 - u, b * (NPR * 16) + (i * 16 if u else (i - 1) * 16))
                    exp_q(g, u)

                step(0, 1)
                with act.Fori(1, NPR) as i:
                    for u in range(2):
                        step(i, u)
                copy_eT(c0 + (NCH - 1), 1)
                copy_qT(c0 + (NCH - 1), 1, b * (NPR * 16) + (NPR - 1) * 16)
                act.wait_ge(s1[6], b + 1)
                act.wait_ge(eT_ps, c0 + NCH + 1)
                with act.Fori(0, NPR) as i:
                    for u in range(2):
                        for h in range(NH):
                            n = i * 4 + 2 * u + h
                            act.wait_ge(ring_used, b * RING + n + 4)
                            act.wait_ge(sq_done, b * (2 * NCH) + n)
                            nc.scalar.activation(junk[:, 0, :], x_sb[:, h, bass.ds(i * (2 * T) + u * T, T)],
                                                 ACT.Square, bias=NB[:, h:h + 1],
                                                 accum_out=sq[:, h, bass.ds(i * 2 + u, 1)]).then_inc(sq_done, 1)
                act.wait_ge(s2[7], b + 1)
                nc.scalar.activation(hid[:, 0, :], ps_qT[:, 8:8 + J], ACT.Exp, scale=-1.0).then_inc(s2[8], 1)
                if last:
                    return
                with act.Fori(0, NQ) as i:
                    for u in range(4):
                        act.wait_ge(out_st[u], b * (NQ * 16) + (i + 1) * 16)
                        act.wait_ge(x_in[u], b * (NQ * 16) + (i + NQ) * 16)
                        load_pair(b + 1, i, u)

            with act.Fori(0, B - 1) as b:
                image(b, False)
            image(B - 1, True)

        @block.tensor
        def _(pe):
            mm = nc.tensor.matmul
            pe.wait_ge(consts, 1)
            for n in range(3):
                pe.wait_ge(w_in[n], 16)
            tr = 0
            for raw_w, blocks in ((wq_raw, 3), (cw_raw, 1), (w1_raw, 2)):
                for h in range(NH):
                    if raw_w is cw_raw:
                        srcs = [cw_raw[:, h, :]]
                    else:
                        srcs = [raw_w[:, t, h * P:(h + 1) * P] for t in range(blocks)]
                    if tr >= 2:
                        pe.wait_ge(w_cp, tr - 1)
                    for t, s in enumerate(srcs):
                        last = nc.tensor.transpose(PS[:, tr % 2, t * P:(t + 1) * P], s, ident[:, :])
                    last.then_inc(w_tr, 1)
                    tr += 1
            pe.wait_ge(w_cp, 6)
            pe.sem_inc(cg_ready, 1)
            pe.sem_inc(eT_ps, 1)
            pe.sem_inc(ring_full, 4)

            def products(g, u):
                pe.wait_ge(xn_ready, g + 1)
                pe.wait_ge(ek_ready, g)
                for h in range(NH):
                    last = mm(ps_k, wqvk[:, h, 2 * HID:3 * HID], xn[:, u, h, :], start=(h == 0), stop=(h == NH - 1))
                last.then_inc(k_ready, 1)
                pe.wait_ge(v_ready, g)
                pe.wait_ge(q_shift, g)
                for t in range(NT):
                    for h in range(NH):
                        last = mm(ps_qv[u][:, t, :], xn[:, u, h, t * P:(t + 1) * P], wqvk[:, h, 0:2 * HID],
                                  start=(h == 0), stop=(h == NH - 1))
                last.then_inc(qv_ready, 1)

            def contexts(g, u):
                pe.wait_ge(ek_ready, g + 1)
                pe.wait_ge(eT_sb, g)
                for t in range(NT):
                    last = nc.tensor.transpose(ps_eT[:, t * P:(t + 1) * P], e_k[:, u, t * P:(t + 1) * P], ident[:, :])
                last.then_inc(eT_ps, 1)
                pe.wait_ge(qn_ready, g + 2)
                pe.wait_ge(qT_sb, g)
                for t in range(NT):
                    last = nc.tensor.transpose(ps_qT[:, t * P:(t + 1) * P], qn[:, u, t, 0:HID], ident[:, :])
                last.then_inc(qT_ps, 1)
                pe.wait_ge(cg_used, g + 1)
                for t in range(NT):
                    mm(ps_cg[:, G1:2 * G1], qn[:, u, t, 0:HID], qn[:, u, t, :], start=(t == 0), stop=(t == NT - 1))
                pe.wait_ge(eT_sb, g + 1)
                pe.wait_ge(v_ready, g + 2)
                for t in range(NT):
                    last = mm(ps_cg[:, 0:G1], e_kT[:, t, :], v_sb[:, u, t, :], start=(t == 0), stop=(t == NT - 1))
                last.then_inc(cg_ready, 1)

            with pe.Fori(0, B) as b:
                pe.wait_ge(s0[0], b + 1)
                mm(ps_cg[:, 0:NH], group[:, :], mv[:, :, 0], start=True, stop=True).then_inc(s0[1], 1)
                pe.wait_ge(s0[2], b + 1)
                mm(ps_cg[:, 8:8 + NH], group[:, :], SVAR, start=True, stop=True).then_inc(s0[3], 1)
                c0 = b * NCH
                products(c0, 0)
                with pe.Fori(0, NPR - 1) as i:
                    products(c0 + i * 2 + 1, 1)
                    contexts(c0 + i * 2, 0)
                    products(c0 + i * 2 + 2, 0)
                    contexts(c0 + i * 2 + 1, 1)
                products(c0 + (NCH - 1), 1)
                contexts(c0 + (NCH - 2), 0)
                contexts(c0 + (NCH - 1), 1)
                pe.wait_ge(s1[0], b + 1)
                pe.wait_ge(qT_sb, c0 + NCH)
                mm(ps_qT[:, 0:C], ctxm[:, :], convT[:, :], start=True, stop=True).then_inc(s1[1], 1)
                pe.wait_ge(s1[2], b + 1)
                mm(ps_eT[:, 0:C], gs[:, 0:HID], MT[:, :], start=True, stop=True)
                for h in range(NH):
                    last = mm(ps_qT[:, C + h:C + h + 1], MT[:, h * P:(h + 1) * P], gs[:, HID:G1], start=True, stop=True)
                last.then_inc(s1[3], 1)
                pe.wait_ge(s1[4], b + 1)
                for h in range(NH):
                    last = mm(ps_qT[:, C + 4 + h:C + 5 + h], pz[:, h * P:(h + 1) * P], ones[:, 0:1], start=True, stop=True)
                last.then_inc(s1[5], 1)
                with pe.Fori(0, NPR // 2) as i:
                    for v in range(2):
                        pe.wait_ge(q_in[v], b * (NPR * 8) + i * 16 + 16)
                        for u in range(2):
                            for h in range(NH):
                                n = 2 * u + h
                                pe.wait_ge(ring_used, b * RING + i * 8 + 4 * v + n)
                                mm(ring[n], MT[:, h * P:(h + 1) * P], ql[:, v, u * T:(u + 1) * T],
                                   start=True, stop=True).then_inc(ring_full, 1)
                pe.wait_ge(s2[0], b + 1)
                mm(ps_cg[:, 0:NH], group[:, :], MEAN1, start=True, stop=True).then_inc(s2[1], 1)
                pe.wait_ge(s2[2], b + 1)
                mm(ps_cg[:, 8:8 + NH], group[:, :], SVAR, start=True, stop=True).then_inc(s2[3], 1)
                pe.wait_ge(s2[6], b + 1)
                for h in range(NH):
                    last = mm(ps_qT[:, 8:8 + J], pooled[:, h, :], se1T[:, h, :], start=(h == 0), stop=(h == NH - 1))
                last.then_inc(s2[7], 1)
                pe.wait_ge(s2[9], b + 1)
                for o in range(NH):
                    for h in range(NH):
                        last = mm(ps_cg[:, 16 + o:17 + o], WB[:, h, o * P:(o + 1) * P], VEC[:, h:h + 1],
                                  start=(h == 0), stop=(h == NH - 1))
                last.then_inc(s2[10], 1)
                with pe.Fori(0, NPR) as i:
                    for u in range(2):
                        for o in range(NH):
                            n = 2 * u + o
                            pe.wait_ge(ring_used, b * RING + (2 * NCH) + i * 4 + n)
                            for h in range(NH):
                                last = mm(ring[n], WS[:, h, o * P:(o + 1) * P],
                                          x_sb[:, h, bass.ds(i * (2 * T) + u * T, T)],
                                          start=(h == 0), stop=(h == NH - 1))
                            last.then_inc(ring_full, 1)

        @block.vector
        def _(dve):
            v_ = nc.vector
            tr = 0
            for dst in (wqvk[:, 0, :], wqvk[:, 1, :], convT[:, 0:P], convT[:, P:C], w1T[:, 0, :], w1T[:, 1, :]):
                dve.wait_ge(w_tr, tr + 1)
                if tr < 2:
                    for t, c in ((0, 0), (1, 2), (2, 1)):
                        last = v_.tensor_copy(dst[:, c * HID:(c + 1) * HID], PS[:, tr % 2, t * P:(t + 1) * P])
                else:
                    last = v_.tensor_copy(dst, PS[:, tr % 2, 0:dst.shape[1]])
                last.then_inc(w_cp, 1)
                tr += 1
            dve.drain()
            for s, n in ((v_ready, 1), (q_shift, 1), (ring_used, 3), (cg_used, 1)):
                dve.sem_inc(s, n)
            dve.wait_ge(consts, 1)
            dve.wait_ge(w_in[3], 80)

            def stats(b, i, u):
                dve.wait_ge(x_in[u], b * (NQ * 16) + i * 16 + 16)
                for k in range(2):
                    for h in range(NH):
                        v_.bn_stats(bn[:, h, bass.ds(i * 8 + (2 * u + k), 1), :].rearrange("p a s -> p (a s)"),
                                    x_sb[:, h, bass.ds(i * (8 * T) + (2 * u + k) * T, T)])

            def normalise(g, c, u):
                dve.wait_ge(qv_ready, g)
                for h in range(NH):
                    last = v_.tensor_scalar(xn[:, u, h, :], x_sb[:, h, bass.ds(c, T)], RR[:, h:h + 1],
                                            TT[:, h:h + 1], ALU.mult, ALU.add)
                last.then_inc(xn_ready, 1)

            def maxima(g, u):
                dve.wait_ge(k_ready, g + 1)
                v_.tensor_reduce(negk[:, :], ps_k, axis=AXX, op=ALU.max, negate=True)
                dve.drain()
                dve.wait_ge(alpha_ready, g)
                v_.tensor_tensor(negmax[:, u:u + 1], negmax[:, 1 - u:2 - u], negk[:, :], ALU.min)\
                    .then_inc(negmax_ready, 1)
                dve.wait_ge(qv_ready, g + 2)
                q4 = ps_qv[u][:, :, 0:HID].rearrange("p t (e d) -> p t e d", d=DH)
                qm4 = qm[:, :].rearrange("p (t e) -> p t e", e=HEADS)
                v_.tensor_reduce(qm4, q4, axis=AXX, op=ALU.max)
                dve.drain()
                dve.wait_ge(qn_ready, g)
                v_.tensor_tensor(q_sb[:, u, :, :].rearrange("p (t e) d -> p t e d", e=HEADS), q4,
                                 qm4[:, :, :, None].to_broadcast([P, NT, HEADS, DH]), ALU.subtract)\
                    .then_inc(q_shift, 1)

            def accumulate(g, u):
                dve.wait_ge(cg_ready, g + 2)
                dve.wait_ge(alpha_ready, g + 1)
                v_.scalar_tensor_tensor(acc[:, :], acc[:, :], alpha[:, u:u + 1], ps_cg[:, 0:G1], ALU.mult, ALU.add)
                v_.tensor_tensor(gram[:, :], gram[:, :], ps_cg[:, G1:2 * G1], ALU.add).then_inc(cg_used, 1)

            def sums(g, u):
                dve.wait_ge(q_exp, g + 1)
                v_.tensor_reduce(qsum[:, :], q_sb[:, u, :, :], axis=AXX, op=ALU.add)
                dve.drain()
                v_.reciprocal(qinv[:, u, :], qsum[:, :]).then_inc(q_inv, 1)

            dve.sem_inc(qn_ready, 1)
            dve.sem_inc(qv_ready, 1)

            def final(b, i, u):
                for k in range(2):
                    dve.wait_ge(ring_full, b * RING + i * 16 + (2 * NCH + 4 * u + 2 * k + 2) + 4)
                    for h in range(NH):
                        xc = x_sb[:, h, bass.ds(i * (8 * T) + (2 * u + k) * T, T)]
                        v_.scalar_tensor_tensor(xc, ring[2 * k + h], DD[:, h:h + 1], xc, ALU.add, ALU.add)\
                            .then_inc(ring_used, 1)

            def image(b, last):
                c0 = b * NCH
                for u in range(4):
                    stats(b, NQ - 1, u)
                v_.memset(acc[:, :], 0.0)
                v_.memset(gram[:, :], 0.0)
                v_.memset(negmax[:, 1:2], BIG)
                dve.drain()
                for h in range(NH):
                    ins = v_.bn_aggr(mv[:, h, :], bn[:, h, :, :].rearrange("p c s -> p (c s)"))
                ins.then_inc(s0[0], 1)
                dve.drain()
                v_.tensor_scalar(NB, mv[:, :, 0], -1.0, None, ALU.mult)
                dve.wait_ge(s0[1], b + 1)
                v_.tensor_tensor(DEV, mv[:, :, 0], ps_cg[:, 0:NH], ALU.subtract)
                dve.drain()
                v_.tensor_tensor(D2, DEV, DEV, ALU.mult)
                dve.drain()
                v_.tensor_tensor(SVAR, mv[:, :, 1], D2, ALU.add).then_inc(s0[2], 1)
                dve.wait_ge(s0[3], b + 1)
                v_.tensor_scalar(S1, ps_cg[:, 8:8 + NH], EPS, None, ALU.add).then_inc(s0[4], 1)
                v_.tensor_copy(TT, ps_cg[:, 0:NH])
                dve.drain()
                dve.wait_ge(s0[5], b + 1)
                v_.scalar_tensor_tensor(TT, TT, -1.0, RR, ALU.mult, ALU.mult)
                dve.drain()
                normalise(c0, 0, 0)

                def step(i, u):
                    g = c0 + i * 2 + u
                    normalise(g + 1, i * (2 * T) + (u + 1) * T, 1 - u)
                    maxima(g, u)
                    accumulate(g - 1 if isinstance(i, int) else (c0 + i * 2 if u else c0 + (i - 1) * 2 + 1), 1 - u)
                    sums(g, u)

                normalise(c0 + 1, T, 1)
                maxima(c0, 0)
                sums(c0, 0)
                with dve.Fori(0, NPR - 1) as i:
                    g = c0 + i * 2
                    normalise(g + 2, i * (2 * T) + 2 * T, 0)
                    maxima(g + 1, 1)
                    accumulate(g, 0)
                    sums(g + 1, 1)
                    normalise(g + 3, i * (2 * T) + 3 * T, 1)
                    maxima(g + 2, 0)
                    accumulate(g + 1, 1)
                    sums(g + 2, 0)
                maxima(c0 + (NCH - 1), 1)
                accumulate(c0 + (NCH - 2), 0)
                sums(c0 + (NCH - 1), 1)
                dve.drain()
                accumulate(c0 + (NCH - 1), 1)
                dve.drain()
                v_.reciprocal(DEV[:, 0:1], acc[:, HID:G1])
                v_.tensor_scalar(gs[:, :], gram[:, :], 1.0 / N, None, ALU.mult)
                dve.drain()
                v_.scalar_tensor_tensor(ctxm[:, :], acc[:, 0:HID], DEV[:, 0:1], headmask[:, :], ALU.mult, ALU.mult)\
                    .then_inc(s1[0], 1)
                dve.wait_ge(s1[1], b + 1)
                v_.tensor_copy(MT[:, :], ps_qT[:, 0:C]).then_inc(s1[2], 1)
                dve.wait_ge(s1[3], b + 1)
                v_.tensor_copy(DELTA, ps_qT[:, C:C + NH])
                dve.drain()
                v_.tensor_tensor(pz[:, :], MT[:, :], ps_eT[:, 0:C], ALU.mult).then_inc(s1[4], 1)
                v_.tensor_tensor(D2, DELTA, DELTA, ALU.mult)
                dve.drain()
                dve.wait_ge(s1[5], b + 1)
                v_.tensor_tensor(VAR1, ps_qT[:, C + 4:C + 4 + NH], D2, ALU.subtract)
                dve.drain()
                v_.tensor_scalar(VB, VAR1, 0.0, EPS, ALU.max, ALU.add).then_inc(s1[6], 1)
                v_.tensor_tensor(TT, vecs[:, 0, :], DELTA, ALU.add)
                dve.wait_ge(s1[7], b + 1)
                v_.tensor_tensor(A, RS, vecs[:, 1, :], ALU.mult)
                dve.drain()
                v_.tensor_tensor(TT, vecs[:, 0, :], TT, ALU.subtract)
                v_.tensor_tensor(AD, A, DELTA, ALU.mult)
                dve.drain()
                v_.tensor_tensor(CC, TT, A, ALU.mult)
                v_.tensor_tensor(MEAN1, mv[:, :, 0], AD, ALU.add)
                dve.drain()
                v_.tensor_tensor(CC, CC, vecs[:, 2, :], ALU.add)
                dve.drain()
                v_.tensor_tensor(MEAN1, MEAN1, CC, ALU.add)
                v_.tensor_tensor(D2, AD, AD, ALU.mult)
                with dve.Fori(0, NPR) as i:
                    for u in range(2):
                        for h in range(NH):
                            n = 2 * u + h
                            dve.wait_ge(ring_full, b * RING + i * 4 + n + 5)
                            xc = x_sb[:, h, bass.ds(i * (2 * T) + u * T, T)]
                            v_.scalar_tensor_tensor(xc, ring[n], A[:, h:h + 1], xc, ALU.mult, ALU.add)\
                                .then_inc(ring_used, 1)
                dve.drain()
                dve.wait_ge(s1[6], b + 1)
                ins = v_.tensor_copy(TT, MEAN1)
                ins.then_inc(s2[0], 1)
                dve.wait_ge(sq_done, (b + 1) * (2 * NCH))
                v_.tensor_reduce(SQS, sq[:, :, :], axis=AXX, op=ALU.add)
                dve.drain()
                v_.scalar_tensor_tensor(VAR1, SQS, 1.0 / N, D2, ALU.mult, ALU.subtract)
                dve.wait_ge(s2[1], b + 1)
                v_.tensor_tensor(DEV1, MEAN1, ps_cg[:, 0:NH], ALU.subtract)
                v_.tensor_tensor(VEC, CC, ps_cg[:, 0:NH], ALU.subtract)
                dve.drain()
                v_.tensor_tensor(D2, DEV1, DEV1, ALU.mult)
                dve.drain()
                v_.tensor_tensor(SVAR, VAR1, D2, ALU.add).then_inc(s2[2], 1)
                dve.wait_ge(s2[3], b + 1)
                v_.tensor_scalar(S1, ps_cg[:, 8:8 + NH], EPS, None, ALU.add).then_inc(s2[4], 1)
                dve.wait_ge(s2[5], b + 1)
                v_.tensor_tensor(POOL, DEV1, R1, ALU.mult)
                v_.tensor_tensor(VEC, VEC, R1, ALU.mult)
                dve.drain()
                for h in range(NH):
                    ins = v_.tensor_scalar(pooled[:, h, :], ones[:, :], POOL[:, h:h + 1], None, ALU.mult)
                ins.then_inc(s2[6], 1)
                dve.wait_ge(s2[8], b + 1)
                v_.tensor_scalar(hid[:, 1, :], hid[:, 0, :], 1.0, None, ALU.add)
                dve.drain()
                v_.reciprocal(hid[:, 2, :], hid[:, 1, :])
                dve.drain()
                v_.tensor_tensor(hid[:, 3, :], ps_qT[:, 8:8 + J], hid[:, 2, :], ALU.mult)
                dve.drain()
                dve.wait_ge(se_in, 16 * NH)
                wb = WB[:, :, :].rearrange("p h o -> p (h o)")
                se = se_out[:, :, :, :].rearrange("p h o j -> p (h o) j")
                for j in range(J):
                    ins = v_.scalar_tensor_tensor(
                        wb, se[:, :, j], hid[:, 3, j:j + 1],
                        w1T[:, :, :].rearrange("p h o -> p (h o)") if j == 0 else wb, ALU.mult, ALU.add)
                    dve.drain()
                for h in range(NH):
                    ins = v_.tensor_scalar(WS[:, h, :], WB[:, h, :], R1[:, h:h + 1], None, ALU.mult)
                ins.then_inc(s2[9], 1)
                dve.wait_ge(s2[10], b + 1)
                v_.tensor_tensor(DD, CC, ps_cg[:, 16:16 + NH], ALU.add)
                dve.drain()
                for u in range(4):
                    final(b, 0, u)
                with dve.Fori(0, NQ - 1) as i:
                    for u in range(4):
                        final(b, i + 1, u)
                        if not last:
                            stats(b + 1, i, u)
                dve.drain()

            with dve.Fori(0, NQ - 1) as i:
                for u in range(4):
                    stats(0, i, u)
            with dve.Fori(0, B - 1) as b:
                image(b, False)
            image(B - 1, True)


_INS = ["x", "L0_conv_qkv_w", "L0_conv_conv_w", "L0_conv_conv_b", "L0_conv_gamma", "L0_conv_beta",
        "L1_conv_w_conv", "L1_conv_w_se1", "L1_conv_w_se_out"]


def kernel(**inputs):
    import numpy as _np
    import concourse.bacc as _bacc
    from concourse import mybir as _mybir
    from concourse.bass_utils import run_bass_kernel_spmd as _run

    nc = _bacc.Bacc("TRN2", target_bir_lowering=False, num_devices=1)
    arrays, args = {}, []
    for name in _INS:
        a = _np.ascontiguousarray(inputs[name])
        arrays[f"in_{name}"] = a
        args.append(nc.dram_tensor(f"in_{name}", a.shape, _mybir.dt.from_np(a.dtype), kind="ExternalInput").ap())
    shape = arrays["in_x"].shape
    args.append(nc.dram_tensor("out_x2", shape, _mybir.dt.float32, kind="ExternalOutput").ap())
    block_program(nc, *args)
    r = _run(nc, [arrays], core_ids=[0])
    return r.results[0]["out_x2"]
```

```python
import concourse.bass as bass
from concourse import mybir
from contextlib import ExitStack

F32 = mybir.dt.float32
F32R = mybir.dt.float32r
ALU = mybir.AluOpType
ACT = mybir.ActivationFunctionType
AXX = mybir.AxisListType.X

P = 128
HEADS, DH = 4, 32
HID = HEADS * DH
GC = 8
T = 512
NT = T // P
EPS = 1e-5
BIG = 3.0e38


def block_program(nc, x, qkv_w, conv_w, conv_b, gamma, beta, w_conv, w_se1, w_se_out, out):
    B, C, H, W = x.shape
    N = H * W
    NH = C // P
    NCH = N // T
    NPR = NCH // 2
    NQ = NPR // 4
    J = w_se1.shape[0]
    G1 = HID + 1

    x_v = x.rearrange("b (h p) r w -> b p h (r w)", p=P)
    out_v = out.rearrange("b (h p) r w -> b p h (r w)", p=P)
    q_dram = nc.dram_tensor("q_dram", (B, P, N), F32, kind="Internal").ap()
    se_dram = nc.dram_tensor("se_dram", (NH, P, C * J), F32, kind="Internal").ap()

    ctx = ExitStack()
    with ctx:
        def sb(name, shape, dtype=F32):
            return ctx.enter_context(nc.sbuf_tensor(name, shape, dtype))

        def sem(name):
            return ctx.enter_context(nc.semaphore(name))

        x_sb = sb("x_sb", [P, NH, N])
        ident = sb("ident", [P, P])
        ones = sb("ones", [P, P])
        group = sb("group", [P, P])
        headmask = sb("headmask", [P, P])
        powers = sb("powers", [P, NH])
        wqT = sb("wqT", [P, NH, 3 * HID])
        wqvk = sb("wqvk", [P, 2, NH, 3 * HID], F32R)
        convT = sb("convT", [P, C])
        w1T = sb("w1T", [P, NH, C])
        se1T = sb("se1T", [P, NH, J])
        vecs = sb("vecs", [P, 3, NH])
        work = sb("work", [P, 8 * T])
        e_k = work[:, 0:2 * T].rearrange("p (u n) -> p u n", u=2)
        q_sb = work[:, 2 * T:4 * T].rearrange("p (u a d) -> p u a d", u=2, d=DH)
        qT = work[:, 4 * T:6 * T].rearrange("p (u n) -> p u n", u=2)
        e_kT = work[:, 6 * T:7 * T].rearrange("p (t c) -> p t c", t=NT)
        q_tok = work[:, 2 * T:4 * T].rearrange("p (u t c) -> p u t c", u=2, t=NT)
        xhl = sb("xhl", [P, 2, 2, NH, T], F32R)
        qhl = sb("qhl", [P, 2, NT, 2, HID], F32R)
        v_sb = sb("v_sb", [P, 2, NT, G1])
        qm = sb("qm", [P, NT * HEADS])
        qsum = sb("qsum", [P, NT * HEADS])
        qinv = sb("qinv", [P, 2, NT * HEADS])
        negk = sb("negk", [P, 1])
        negmax = sb("negmax", [P, 2])
        alpha = sb("alpha", [P, 2])
        acc = sb("acc", [P, G1])
        gram = sb("gram", [P, 2 * HID])
        gram_q = sb("gram_q", [P, HID])
        qs = sb("qs", [P, NCH])
        mu = sb("mu", [P, 2])
        bn = sb("bn", [P, NH, NCH, 6])
        mv = sb("mv", [P, NH, 2])
        sm = sb("sm", [P, 24, NH])
        MT = sb("MT", [P, C])
        ctxm = sb("ctxm", [P, P])
        hid = sb("hid", [P, 4, J])
        sq = sb("sq", [P, NH, NCH])
        WB = sb("WB", [P, NH, C])
        WS = sb("WS", [P, 2, NH, C], F32R)
        ql = sb("ql", [P, 2, 2 * T])
        (DEV, SVAR, RR, NB, DELTA, D2, VB, RS, A, TT, CC, SQS, AD, MEAN1, VAR1, DEV1, S1, R1, POOL,
         VEC, DD, NM) = (sm[:, n, :] for n in range(22))
        se_sb = [xhl[:, :, :, :, :].rearrange("p u s h n -> p (u s h n)").bitcast(F32), work[:, :]]
        stage = ql[:, 1, :].rearrange("p (h n) -> p h n", h=NH)
        prod = [ql[:, n // 2, n % 2 * T:(n % 2 + 1) * T] for n in range(3)]
        wsum = ql[:, 1, T:2 * T]
        pz = sb("pz", [P, C])
        pooled = pz[:, :].rearrange("p (h c) -> p h c", h=NH)
        wq_raw = work[:, 0:3 * C].rearrange("p (t c) -> p t c", t=3)
        cw_raw = work[:, 3 * C:4 * C].rearrange("p (t c) -> p t c", t=NH)
        w1_raw = work[:, 4 * C:6 * C].rearrange("p (t c) -> p t c", t=NH)

        PS = ctx.enter_context(nc.psum_tensor("PS", [P, 8, T], F32))
        ps_k = PS[:, 0, :]
        ps_qv = [PS[:, 1 + 2 * u:3 + 2 * u, :].rearrange("p a (b c) -> p (a b) c", c=2 * HID)
                 for u in range(2)]
        ps_eT, ps_qT, ps_cg = PS[:, 5, :], PS[:, 6, :], PS[:, 7, :]
        ring = [PS[:, 1 + n, :] for n in range(4)]

        w_in = [sem(f"w_in{n}") for n in range(4)]
        se_out = [sem(f"se_out{n}") for n in range(NH)]
        se_in = [sem(f"se_in{n}") for n in range(NH)]
        pool_step, consts = sem("pool_step"), sem("consts")
        w_tr, w_cp = sem("w_tr"), sem("w_cp")
        x_in = [sem(f"x_in{n}") for n in range(4)]
        out_st = [sem(f"out_st{n}") for n in range(4)]
        q_st = [sem(f"q_st{n}") for n in range(2)]
        q_in = [sem(f"q_in{n}") for n in range(2)]
        stage_in = [sem(f"stage_in{n}") for n in range(NH)]
        stage_used = sem("stage_used")
        sp_passed = sem("sp_passed")
        xh_ready, xl_ready = sem("xh_ready"), sem("xl_ready")
        k_ready, qv_ready = sem("k_ready"), sem("qv_ready")
        negmax_ready, ek_ready, alpha_ready = sem("negmax_ready"), sem("ek_ready"), sem("alpha_ready")
        q_shift, q_exp, q_inv, qn_ready = sem("q_shift"), sem("q_exp"), sem("q_inv"), sem("qn_ready")
        v_ready, eT_ps, eT_sb = sem("v_ready"), sem("eT_ps"), sem("eT_sb")
        qh_ready, ql_ready = sem("qh_ready"), sem("ql_ready")
        qT_ps, qT_sb, cg_ready, cg_used = sem("qT_ps"), sem("qT_sb"), sem("cg_ready"), sem("cg_used")
        x1h_ready, x1l_ready = sem("x1h_ready"), sem("x1l_ready")
        x1_used = sem("x1_used")
        ring_full, ring_used, sq_done = sem("ring_full"), sem("ring_used"), sem("sq_done")
        s0 = [sem(f"s0_{n}") for n in range(8)]
        wh_ready, ctx_end = sem("wh_ready"), sem("ctx_end")
        s1 = [sem(f"s1_{n}") for n in range(9)]
        hid_ready, prod_ready, prod_used = sem("hid_ready"), sem("prod_ready"), sem("prod_used")
        wb_step = sem("wb_step")
        s2 = [sem(f"s2_{n}") for n in range(12)]

        block = ctx.enter_context(nc.Block())
        JP = 6
        JD = J - JP
        PARTS = ((0, 0), (0, 1), (1, 0))
        RING = 2 * 2 * NCH

        @block.sync
        def _(sp):
            for s in (*x_in, *out_st, *q_st, *se_out):
                sp.sem_inc(s, 16)
            sp.dma_start(wq_raw, qkv_w.rearrange("(t p) c -> p t c", p=P)).then_inc(w_in[0], 16)
            sp.dma_start(cw_raw, conv_w.rearrange("(t p) c -> p t c", p=P)).then_inc(w_in[1], 16)
            sp.dma_start(w1_raw, w_conv.rearrange("(t p) c i j -> p t (c i j)", p=P)).then_inc(w_in[2], 16)
            def load_pair(b, i, u):
                sp.dma_start(x_sb[:, :, bass.ds(i * (8 * T) + u * (2 * T), 2 * T)],
                             x_v[b, :, :, bass.ds(i * (8 * T) + u * (2 * T), 2 * T)]).then_inc(x_in[u], 16)

            with sp.Fori(0, NQ) as i:
                for u in range(4):
                    sp.wait_ge(x_in[u], i * 16 + 16)
                    load_pair(0, i, u)
            with nc.allow_non_contiguous_dma("vectors and the squeeze weights, once"):
                for n, v in enumerate((conv_b, gamma, beta)):
                    sp.dma_start(vecs[:, n, :], v.rearrange("(h p) -> p h", p=P)).then_inc(w_in[3], 16)
                    sp.wait_ge(w_in[3], 16 * (n + 1))
                for h in range(NH):
                    sp.dma_start(se1T[:, h, :], w_se1[:, h * P:(h + 1) * P].rearrange("j p -> p j")).then_inc(w_in[3], 16)
                    sp.wait_ge(w_in[3], 16 * (h + 4))

            def store_pair(b, i, u):
                sp.wait_ge(ring_used, b * RING + i * 16 + (2 * NCH + 4 * (u + 1)) + 4)
                sp.sem_inc(sp_passed, 1)
                sp.wait_ge(out_st[u], b * (NQ * 16) + i * 16 + 16)
                sp.sem_inc(sp_passed, 1)
                sp.dma_start(out_v[b, :, :, bass.ds(i * (8 * T) + u * (2 * T), 2 * T)],
                             x_sb[:, :, bass.ds(i * (8 * T) + u * (2 * T), 2 * T)]).then_inc(out_st[u], 16)

            def load_next(b, i, u):
                sp.wait_ge(out_st[u], b * (NQ * 16) + (i + 1) * 16 + 16)
                sp.sem_inc(sp_passed, 1)
                sp.wait_ge(x_in[u], b * (NQ * 16) + (i + NQ) * 16 + 16)
                sp.sem_inc(sp_passed, 1)
                load_pair(b + 1, i, u)

            def relay(i, h):
                rows = C // NPR
                sp.wait_ge(se_out[h], i * 16 + 16)
                sp.sem_inc(sp_passed, 1)
                with nc.allow_non_contiguous_dma("the squeeze weights, once"):
                    sp.dma_start(se_dram[h].rearrange("p (o j) -> p o j", j=J)[:, bass.ds(i * rows, rows), :],
                                 w_se_out.rearrange("(o h p) j -> h p o j", h=NH, p=P)[h][:, bass.ds(i * rows, rows), :])\
                      .then_inc(se_out[h], 16)

            def image(b, first, last):
                def spill(i, u):
                    sp.wait_ge(qT_sb, b * NCH + i * 2 + u + 2)
                    sp.sem_inc(sp_passed, 1)
                    sp.dma_start(q_dram[b, :, bass.ds(i * (2 * T) + u * T, T)], qT[:, u, :]).then_inc(q_st[u], 16)

                def load_stage(i, h):
                    sp.wait_ge(stage_used, b * NCH + i * 2 + (h - 1))
                    sp.sem_inc(sp_passed, 1)
                    sp.wait_ge(stage_in[h], b * (NPR * 16) + i * 16)
                    sp.sem_inc(sp_passed, 1)
                    sp.dma_start(stage[:, h, :], x_v[b + 1, :, h, bass.ds(i * T + N // 2, T)]).then_inc(stage_in[h], 16)

                with sp.Fori(0, NPR - 1) as i:
                    for u in range(2):
                        spill(i, u)
                        if not last:
                            load_stage(i + 1, u)
                        if first:
                            relay(i, u)
                if first:
                    for u in range(2):
                        relay(NPR - 1, u)

                def load_queries(i, u):
                    sp.wait_ge(ring_full, b * RING + i * 8 + u * 4 + 1)
                    sp.sem_inc(sp_passed, 1)
                    sp.dma_start(ql[:, u, :], q_dram[b, :, bass.ds(i * (4 * T) + u * (2 * T), 2 * T)])\
                      .then_inc(q_in[u], 16)

                for u in range(2):
                    sp.wait_ge(q_st[u], b * (NPR * 16) + (NPR - 1) * 16 + 16)
                sp.sem_inc(sp_passed, 1)
                load_queries(0, 0)
                if not last:
                    sp.wait_ge(stage_used, (b + 1) * NCH)
                    sp.sem_inc(sp_passed, 1)
                load_queries(0, 1)
                for u in range(2):
                    spill(NPR - 1, u)
                for u in range(2):
                    sp.wait_ge(q_st[u], (b + 1) * (NPR * 16) + 16)
                sp.sem_inc(sp_passed, 1)
                for i in range(1, 5):
                    for u in range(2):
                        load_queries(i, u)
                    if i == 1:
                        sp.wait_ge(s1[0], b + 1)
                        sp.sem_inc(sp_passed, 1)
                    h, half = (i - 1) // 2, bass.ds((i - 1) % 2 * (C * J // 2), C * J // 2)
                    sp.wait_ge(se_out[h], NPR * 16 + 16)
                    sp.dma_start(se_sb[h][:, half], se_dram[h][:, half]).then_inc(se_in[h], 16)
                with sp.Fori(5, NPR // 2) as i:
                    for u in range(2):
                        load_queries(i, u)
                if last:
                    with sp.Fori(0, NQ) as i:
                        for u in range(4):
                            store_pair(b, i, u)
                    return
                for u in range(4):
                    store_pair(b, 0, u)
                    if u >= 1:
                        load_next(b, 0, u - 1)
                with sp.Fori(0, NQ - 1) as i:
                    for u in range(4):
                        store_pair(b, i + 1, u)
                        load_next(b, i + (u + 3) // 4, (u + 3) % 4)
                load_next(b, NQ - 1, 3)

            image(0, True, False)
            with sp.Fori(1, B - 1) as b:
                image(b, False, False)
            image(B - 1, False, True)
            for u in range(4):
                sp.wait_ge(out_st[u], B * NQ * 16 + 16)

        @block.gpsimd
        def _(pool):
            steps = [0]

            def step(ins):
                steps[0] += 1
                ins.then_inc(pool_step, 1)
                pool.wait_ge(pool_step, steps[0])

            step(nc.gpsimd.memset(ident[:, :], 0.0))
            step(nc.gpsimd.affine_select(out=ident[:, :], in_=ident[:, :], compare_op=ALU.not_equal, fill=1.0,
                                         base=0, pattern=[[-1, P]], channel_multiplier=1))
            step(nc.gpsimd.memset(ones[:, :], 1.0))
            step(nc.gpsimd.memset(powers[:, :], -0.5))
            step(nc.gpsimd.memset(v_sb[:, :, :, HID:G1], 1.0))
            for tile, size, value in ((group, GC, 1.0 / GC), (headmask, DH, float(DH) ** -0.5 / N)):
                step(nc.gpsimd.memset(tile[:, :], value))
                v = tile[:, :].rearrange("p (g s) -> p g s", s=size)
                step(nc.gpsimd.affine_select(out=v, in_=v, compare_op=ALU.is_ge, fill=0.0, base=0,
                                             pattern=[[-size, P // size], [0, size]], channel_multiplier=1))
                step(nc.gpsimd.affine_select(out=v, in_=v, compare_op=ALU.is_ge, fill=0.0, base=size - 1,
                                             pattern=[[size, P // size], [0, size]], channel_multiplier=-1))
            pool.sem_inc(consts, 1)

            def b0_deviation(b):
                pool.wait_ge(s0[4], b + 1)
                nc.gpsimd.tensor_tensor(RR, S1, powers[:, :], ALU.pow).then_inc(s0[5], 1)

            def image(b, last):
                c0 = b * NCH

                def queries(g, u):
                    pool.wait_ge(q_inv, g + 1)
                    q4 = q_sb[:, u, :, :].rearrange("p (t e) d -> p t e d", e=HEADS)
                    nc.gpsimd.tensor_tensor(
                        q4, q4, qinv[:, u, :].rearrange("p (t e) -> p t e", e=HEADS)[:, :, :, None]
                        .to_broadcast([P, NT, HEADS, DH]), ALU.mult).then_inc(qn_ready, 1)
                    pool.wait_ge(qh_ready, g + 1)
                    nc.gpsimd.tensor_tensor(qhl[:, u, :, 1, :], q_tok[:, u, :, :], qhl[:, u, :, 0, :].bitcast(F32),
                                            ALU.subtract).then_inc(ql_ready, 1)

                with pool.Fori(0, NPR) as i:
                    for u in range(2):
                        queries(c0 + i * 2 + u, u)
                pool.wait_ge(s1[6], b + 1)
                nc.gpsimd.tensor_tensor(RS, VB, powers[:, :], ALU.pow).then_inc(s1[7], 1)
                pool.wait_ge(s2[4], b + 1)
                nc.gpsimd.tensor_tensor(R1, S1, powers[:, :], ALU.pow).then_inc(s2[5], 1)
                for k in range(1, JP):
                    pool.wait_ge(prod_ready, b * JP + k + 1)
                    if k >= 2:
                        pool.wait_ge(prod_used, b * (JP - 1) + k - 1)
                    nc.gpsimd.tensor_tensor(wsum, prod[0] if k == 1 else wsum, prod[k % 3], ALU.add)\
                      .then_inc(prod_used, 1)
                def low(i):
                    for u in range(2):
                        for h in range(NH):
                            pool.wait_ge(x1h_ready, c0 * 2 + i * 4 + 2 * u + h + 1)
                            nc.gpsimd.tensor_tensor(xhl[:, u, 1, h, :], x_sb[:, h, bass.ds(i * (2 * T) + u * T, T)],
                                                    xhl[:, u, 0, h, :].bitcast(F32), ALU.subtract)\
                              .then_inc(x1l_ready, 1)

                if last:
                    with pool.Fori(0, NPR) as i:
                        low(i)
                    return
                with pool.Fori(0, NPR - 1) as i:
                    low(i)
                b0_deviation(b + 1)
                low(NPR - 1)

            b0_deviation(0)
            with pool.Fori(0, B - 1) as b:
                image(b, False)
            image(B - 1, True)

        @block.scalar
        def _(act):
            def high(g, c, u):
                act.wait_ge(qv_ready, g + 1)
                for h in range(NH):
                    nc.scalar.activation(xhl[:, u, 0, h, :], x_sb[:, h, bass.ds(c, T)], ACT.Identity,
                                         bias=NM[:, h:h + 1]).then_inc(xh_ready, 1)

            def exp_k(b, g, u):
                act.wait_ge(negmax_ready, g + 1)
                act.wait_ge(eT_ps, g + 1)
                nc.scalar.activation(e_k[:, u, :], ps_k, ACT.Exp, bias=negmax[:, u:u + 1]).then_inc(ek_ready, 1)
                act.wait_ge(cg_used, g + 1)
                nc.scalar.activation(alpha[:, u:u + 1], negmax[:, 1 - u:2 - u], ACT.Exp, scale=-1.0,
                                     bias=negmax[:, u:u + 1]).then_inc(alpha_ready, 1)

            def copy_v(g, u):
                act.wait_ge(q_shift, g + 2)
                act.wait_ge(cg_ready, g + 1)
                nc.scalar.activation(v_sb[:, u, :, 0:HID], ps_qv[u][:, :, HID:2 * HID], ACT.Copy).then_inc(v_ready, 1)

            def exp_q(g, u):
                act.wait_ge(q_shift, g + 2)
                nc.scalar.activation(q_sb[:, u, :, :], q_sb[:, u, :, :], ACT.Exp).then_inc(q_exp, 1)

            def copy_eT(g):
                act.wait_ge(eT_ps, g + 3)
                act.wait_ge(cg_ready, g + 2)
                nc.scalar.activation(e_kT[:, :, :], ps_eT.rearrange("p (t c) -> p t c", t=NT), ACT.Copy)\
                  .then_inc(eT_sb, 1)

            def high_q(g, u):
                act.wait_ge(qn_ready, g + 1)
                nc.scalar.activation(qhl[:, u, :, 0, :], q_tok[:, u, :, :], ACT.Copy).then_inc(qh_ready, 1)

            def copy_qT(g, c, u, spilled):
                act.wait_ge(qT_ps, g + 1)
                act.wait_ge(q_st[u], spilled + 16)
                nc.scalar.activation(qT[:, u, :], ps_qT, ACT.Copy,
                                     accum_out=qs[:, bass.ds(c, 1)]).then_inc(qT_sb, 1)

            def b0_weights(b):
                act.wait_ge(s0[5], b + 1)
                for h in range(NH):
                    ins = nc.scalar.activation(wqvk[:, 0, h, :], wqT[:, h, :], ACT.Copy, scale=RR[:, h:h + 1])
                ins.then_inc(wh_ready, 1)

            def b0_high(b):
                act.wait_ge(s0[6], b + 1)
                for u in range(2):
                    act.wait_ge(ring_full, b * RING + 2 * u + 3)
                    high(b * NCH + u, u * T, u)

            def image(b, first, last):
                c0 = b * NCH
                st0 = b * (NPR * 16)
                if not last:
                    for h in range(NH):
                        if not first:
                            act.wait_ge(stage_in[h], b * (NPR * 16))
                        act.dma_start(stage[:, h, :], x_v[b + 1, :, h, N // 2:N // 2 + T]).then_inc(stage_in[h], 16)
                exp_k(b, c0, 0)

                def step(c, u, spilled, high_next=True, k_next=True, qT_last=True):
                    g = c0 + c
                    if high_next:
                        high(g + 2, (c + 2) * T, u)
                    exp_q(g, u)
                    copy_v(g, u)
                    if qT_last:
                        copy_qT(g - 1, c - 1, 1 - u, spilled)
                    copy_eT(g)
                    if k_next:
                        exp_k(b, g + 1, 1 - u)
                    high_q(g, u)

                step(0, 0, 0, qT_last=False)
                with act.Fori(0, NPR // 2 - 2) as i:
                    step(i * 2 + 1, 1, st0 + i * 16)
                    step(i * 2 + 2, 0, st0 + i * 16)
                for n in range(4):
                    act.wait_ge(x_in[n], (b + 1) * (NQ * 16) + 16)
                with act.Fori(NPR // 2 - 2, NPR - 2) as i:
                    step(i * 2 + 1, 1, st0 + i * 16)
                    step(i * 2 + 2, 0, st0 + i * 16)
                step(NCH - 3, 1, st0 + (NPR - 2) * 16)
                step(NCH - 2, 0, st0 + (NPR - 2) * 16, high_next=False)
                step(NCH - 1, 1, st0 + (NPR - 1) * 16, high_next=False, k_next=False)
                act.wait_ge(s1[1], b + 1)
                nc.scalar.activation(MT[:, :], ps_eT[:, 0:C], ACT.Copy).then_inc(s1[2], 1)
                copy_qT(c0 + (NCH - 1), NCH - 1, 1, st0 + (NPR - 1) * 16)
                act.wait_ge(s1[6], b + 1)
                with act.Fori(0, NPR) as i:
                    for u in range(2):
                        for h in range(NH):
                            n = i * 4 + 2 * u + h
                            act.wait_ge(ring_used, b * RING + n + 5)
                            act.wait_ge(sq_done, b * (2 * NCH) + n + 1)
                            nc.scalar.activation(ps_k, x_sb[:, h, bass.ds(i * (2 * T) + u * T, T)],
                                                 ACT.Square, bias=NB[:, h:h + 1],
                                                 accum_out=sq[:, h, bass.ds(i * 2 + u, 1)]).then_inc(sq_done, 1)
                act.wait_ge(s2[7], b + 1)
                nc.scalar.activation(hid[:, 0, :], ps_qT[:, 8:8 + J], ACT.Exp, scale=-1.0).then_inc(s2[8], 1)
                act.wait_ge(hid_ready, b + 1)
                for h in range(NH):
                    act.wait_ge(se_in[h], (b + 1) * 32)
                for k in range(JP):
                    if k >= 3:
                        act.wait_ge(prod_used, b * (JP - 1) + k - 2)
                    for h in range(NH):
                        ins = nc.scalar.activation(prod[k % 3][:, h * C:(h + 1) * C],
                                                   se_sb[h].rearrange("p (o j) -> p o j", j=J)[:, :, JD + k],
                                                   ACT.Copy, scale=hid[:, 3, JD + k:JD + k + 1])
                    ins.then_inc(prod_ready, 1)
                def high_x1(i):
                    for u in range(2):
                        for h in range(NH):
                            if h == 0:
                                act.wait_ge(x1_used, c0 + i * 2 + u + 1)
                            else:
                                act.wait_ge(ring_full, b * RING + (2 * NCH) + i * 4 + 2 * u + 3)
                            nc.scalar.activation(xhl[:, u, 0, h, :], x_sb[:, h, bass.ds(i * (2 * T) + u * T, T)],
                                                 ACT.Copy).then_inc(x1h_ready, 1)

                act.wait_ge(s2[9], b + 1)
                if last:
                    with act.Fori(0, NPR) as i:
                        high_x1(i)
                    return
                with act.Fori(0, NPR - 1) as i:
                    high_x1(i)
                b0_weights(b + 1)
                high_x1(NPR - 1)
                b0_high(b + 1)

            b0_weights(0)
            b0_high(0)
            image(0, True, False)
            with act.Fori(1, B - 1) as b:
                image(b, False, False)
            image(B - 1, False, True)

        @block.tensor
        def _(pe):
            mm = nc.tensor.matmul
            pe.wait_ge(consts, 1)
            for n in range(3):
                pe.wait_ge(w_in[n], 16)
            tr = 0
            for raw_w, blocks in ((wq_raw, 3), (cw_raw, 1), (w1_raw, 2)):
                for h in range(NH):
                    if raw_w is cw_raw:
                        srcs = [cw_raw[:, h, :]]
                    else:
                        srcs = [raw_w[:, t, h * P:(h + 1) * P] for t in range(blocks)]
                    if tr >= 2:
                        pe.wait_ge(w_cp, tr - 1)
                    for t, s in enumerate(srcs):
                        last = nc.tensor.transpose(PS[:, tr % 2, t * P:(t + 1) * P], s, ident[:, :])
                    last.then_inc(w_tr, 1)
                    tr += 1
            pe.wait_ge(w_cp, 6)
            pe.sem_inc(cg_ready, 2)
            pe.sem_inc(eT_ps, 2)
            pe.sem_inc(ring_full, 5)
            pe.sem_inc(x1_used, 2)

            def product_k(g, u):
                pe.wait_ge(xl_ready, g + 1)
                pe.wait_ge(ek_ready, g + 1)
                n = 0
                for h in range(NH):
                    for a, b in PARTS:
                        last = mm(ps_k, wqvk[:, a, h, 2 * HID:3 * HID], xhl[:, u, b, h, :],
                                  start=(n == 0), stop=(n == len(PARTS) * NH - 1))
                        n += 1
                last.then_inc(k_ready, 1)

            def product_qv(g, u):
                pe.wait_ge(v_ready, g + 1)
                for t in range(NT):
                    n = 0
                    for h in range(NH):
                        for a, b in PARTS:
                            last = mm(ps_qv[u][:, t, :], xhl[:, u, a, h, t * P:(t + 1) * P], wqvk[:, b, h, 0:2 * HID],
                                      start=(n == 0), stop=(n == len(PARTS) * NH - 1))
                            n += 1
                last.then_inc(qv_ready, 1)

            def transpose_k(g, u):
                pe.wait_ge(ek_ready, g + 2)
                pe.wait_ge(eT_sb, g + 1)
                for t in range(NT):
                    last = nc.tensor.transpose(ps_eT[:, t * P:(t + 1) * P], e_k[:, u, t * P:(t + 1) * P], ident[:, :])
                last.then_inc(eT_ps, 1)

            def context(g, u):
                pe.wait_ge(cg_used, g + 2)
                pe.wait_ge(eT_sb, g + 2)
                pe.wait_ge(v_ready, g + 3)
                for t in range(NT):
                    last = mm(ps_cg[:, 2 * HID:2 * HID + G1], e_kT[:, t, :], v_sb[:, u, t, :],
                              start=(t == 0), stop=(t == NT - 1))
                return last

            def transpose_q(g, u):
                pe.wait_ge(qn_ready, g + 1)
                pe.wait_ge(qT_sb, g + 1)
                for t in range(NT):
                    last = nc.tensor.transpose(ps_qT[:, t * P:(t + 1) * P], q_tok[:, u, t, :], ident[:, :])
                last.then_inc(qT_ps, 1)

            def gram_matrix(g, u):
                pe.wait_ge(ql_ready, g + 1)
                for t in range(NT):
                    last = mm(ps_cg[:, 0:2 * HID], qhl[:, u, t, 0, :], qhl[:, u, t, :, :].rearrange("p s c -> p (s c)"),
                              start=(t == 0), stop=(t == NT - 1))
                last.then_inc(cg_ready, 1)

            def step(g, u):
                product_k(g, u)
                transpose_k(g - 1, 1 - u)
                product_qv(g, u)
                context(g - 1, 1 - u)
                transpose_q(g - 1, 1 - u)
                gram_matrix(g - 1, 1 - u)

            def mixed(b, i, v, u, h):
                n = 2 * u + h
                pe.wait_ge(ring_used, b * RING + i * 8 + 4 * v + n + 1)
                mm(ring[n], MT[:, h * P:(h + 1) * P], ql[:, v, u * T:(u + 1) * T],
                   start=True, stop=True).then_inc(ring_full, 1)

            def b0_means(b):
                pe.wait_ge(s0[0], b + 1)
                mm(ps_cg[:, 0:NH], group[:, :], mv[:, :, 0], start=True, stop=True).then_inc(s0[1], 1)

            def b0_variances(b):
                pe.wait_ge(s0[2], b + 1)
                mm(ps_cg[:, 8:8 + NH], group[:, :], SVAR, start=True, stop=True).then_inc(s0[3], 1)

            def image(b, last):
                c0 = b * NCH
                pe.wait_ge(s0[7], b + 1)
                product_k(c0, 0)
                pe.wait_ge(ring_used, b * RING + 4)
                product_qv(c0, 0)
                with pe.Fori(0, NPR - 1) as i:
                    for u in range(2):
                        step(c0 + i * 2 + u + 1, 1 - u)
                step(c0 + (NCH - 1), 1)
                transpose_k(c0 + (NCH - 1), 1)
                context(c0 + (NCH - 1), 1).then_inc(ctx_end, 1)
                pe.wait_ge(s1[0], b + 1)
                mm(ps_eT[:, 0:C], ctxm[:, :], convT[:, :], start=True, stop=True).then_inc(s1[1], 1)
                transpose_q(c0 + (NCH - 1), 1)
                gram_matrix(c0 + (NCH - 1), 1)
                pe.wait_ge(q_in[0], b * (NPR * 8) + 16)
                pe.wait_ge(s1[2], b + 1)
                mixed(b, 0, 0, 0, 0)
                pe.wait_ge(s1[8], b + 1)
                mm(ps_qT[:, 0:C], gram_q[:, :], MT[:, :], start=True, stop=True)
                for h in range(NH):
                    ins = mm(ps_qT[:, C + h:C + h + 1], MT[:, h * P:(h + 1) * P], mu[:, 1:2], start=True, stop=True)
                ins.then_inc(s1[3], 1)
                mixed(b, 0, 0, 0, 1)
                pe.wait_ge(s1[4], b + 1)
                for h in range(NH):
                    ins = mm(ps_qT[:, C + 4 + h:C + 5 + h], pz[:, h * P:(h + 1) * P], ones[:, 0:1], start=True, stop=True)
                ins.then_inc(s1[5], 1)
                for h in range(NH):
                    mixed(b, 0, 0, 1, h)
                def mixed_pair(i, v):
                    pe.wait_ge(q_in[v], b * (NPR * 8) + i * 16 + 16)
                    for u in range(2):
                        for h in range(NH):
                            mixed(b, i, v, u, h)

                mixed_pair(0, 1)
                with pe.Fori(1, NPR // 2) as i:
                    for v in range(2):
                        mixed_pair(i, v)
                pe.wait_ge(s2[0], b + 1)
                mm(ps_cg[:, 0:NH], group[:, :], MEAN1, start=True, stop=True).then_inc(s2[1], 1)
                pe.wait_ge(s2[2], b + 1)
                mm(ps_cg[:, 8:8 + NH], group[:, :], SVAR, start=True, stop=True).then_inc(s2[3], 1)
                pe.wait_ge(s2[6], b + 1)
                for h in range(NH):
                    ins = mm(ps_qT[:, 8:8 + J], pooled[:, h, :], se1T[:, h, :], start=(h == 0), stop=(h == NH - 1))
                ins.then_inc(s2[7], 1)
                pe.wait_ge(s2[9], b + 1)
                for o in range(NH):
                    for h in range(NH):
                        ins = mm(ps_cg[:, 16 + o:17 + o], WB[:, h, o * P:(o + 1) * P], VEC[:, h:h + 1],
                                 start=(h == 0), stop=(h == NH - 1))
                ins.then_inc(s2[10], 1)
                def final_pair(i):
                    for u in range(2):
                        for o in range(NH):
                            pe.wait_ge(ring_used, b * RING + (2 * NCH) + i * 4 + 2 * u + o + 1)
                        for h in range(NH):
                            pe.wait_ge(x1l_ready, c0 * 2 + i * 4 + 2 * u + h + 1)
                            for o in range(NH):
                                for m, (a, c) in enumerate(PARTS):
                                    last_mm = mm(ring[2 * u + o], WS[:, a, h, o * P:(o + 1) * P], xhl[:, u, c, h, :],
                                                 start=(h == 0 and m == 0), stop=(h == NH - 1 and m == len(PARTS) - 1))
                                if h == NH - 1:
                                    last_mm.then_inc(ring_full, 1)
                                elif o == NH - 1:
                                    last_mm.then_inc(x1_used, 1)

                if last:
                    with pe.Fori(0, NPR) as i:
                        final_pair(i)
                    return
                with pe.Fori(0, NPR - 3) as i:
                    final_pair(i)
                b0_means(b + 1)
                final_pair(NPR - 3)
                b0_variances(b + 1)
                for i in range(NPR - 2, NPR):
                    final_pair(i)

            b0_means(0)
            b0_variances(0)
            with pe.Fori(0, B - 1) as b:
                image(b, False)
            image(B - 1, True)

        @block.vector
        def _(dve):
            v_ = nc.vector
            tr = 0
            for dst in (wqT[:, 0, :], wqT[:, 1, :], convT[:, 0:P], convT[:, P:C], w1T[:, 0, :], w1T[:, 1, :]):
                dve.wait_ge(w_tr, tr + 1)
                if tr < 2:
                    for t, c in ((0, 0), (1, 2), (2, 1)):
                        last = v_.tensor_copy(dst[:, c * HID:(c + 1) * HID], PS[:, tr % 2, t * P:(t + 1) * P])
                else:
                    last = v_.tensor_copy(dst, PS[:, tr % 2, 0:dst.shape[1]])
                last.then_inc(w_cp, 1)
                tr += 1
            dve.drain()
            for s, n in ((v_ready, 2), (q_shift, 1), (ring_used, 4), (cg_used, 2), (qv_ready, 2),
                         (ek_ready, 1), (eT_sb, 1), (qT_sb, 1), (alpha_ready, 1), (sq_done, 1)):
                dve.sem_inc(s, n)
            dve.wait_ge(consts, 1)

            def stats(b, i, u):
                dve.wait_ge(x_in[u], b * (NQ * 16) + i * 16 + 32)
                for k in range(2):
                    for h in range(NH):
                        v_.bn_stats(bn[:, h, bass.ds(i * 8 + (2 * u + k), 1), :].rearrange("p a s -> p (a s)"),
                                    x_sb[:, h, bass.ds(i * (8 * T) + (2 * u + k) * T, T)])

            def low(g, c, u, h):
                dve.wait_ge(xh_ready, 2 * g + (h + 1))
                ins = v_.scalar_tensor_tensor(xhl[:, u, 1, h, :], x_sb[:, h, bass.ds(c, T)], NM[:, h:h + 1],
                                              xhl[:, u, 0, h, :].bitcast(F32), ALU.add, ALU.subtract)
                if h == NH - 1:
                    ins.then_inc(xl_ready, 1)

            def maximum_k(g, u):
                dve.wait_ge(k_ready, g + 1)
                v_.tensor_reduce(negk[:, :], ps_k, axis=AXX, op=ALU.max, negate=True)
                dve.drain()
                dve.wait_ge(alpha_ready, g + 1)
                v_.tensor_tensor(negmax[:, u:u + 1], negmax[:, 1 - u:2 - u], negk[:, :], ALU.min)\
                    .then_inc(negmax_ready, 1)

            def maximum_q(g, u):
                dve.wait_ge(qv_ready, g + 3)
                q4 = ps_qv[u][:, :, 0:HID].rearrange("p t (e d) -> p t e d", d=DH)
                qm4 = qm[:, :].rearrange("p (t e) -> p t e", e=HEADS)
                v_.tensor_reduce(qm4, q4, axis=AXX, op=ALU.max)
                dve.drain()
                v_.tensor_tensor(q_sb[:, u, :, :].rearrange("p (t e) d -> p t e d", e=HEADS), q4,
                                 qm4[:, :, :, None].to_broadcast([P, NT, HEADS, DH]), ALU.subtract)\
                    .then_inc(q_shift, 1)

            def accumulate(g, u):
                dve.wait_ge(cg_ready, g + 3)
                dve.wait_ge(alpha_ready, g + 2)
                v_.scalar_tensor_tensor(acc[:, :], acc[:, :], alpha[:, u:u + 1], ps_cg[:, 2 * HID:2 * HID + G1],
                                        ALU.mult, ALU.add)
                v_.tensor_tensor(gram[:, :], gram[:, :], ps_cg[:, 0:2 * HID], ALU.add).then_inc(cg_used, 1)

            def sums(g, u):
                dve.wait_ge(q_exp, g + 1)
                v_.tensor_reduce(qsum[:, :], q_sb[:, u, :, :], axis=AXX, op=ALU.add)
                dve.drain()
                v_.reciprocal(qinv[:, u, :], qsum[:, :]).then_inc(q_inv, 1)


            def final(b, i, u, k):
                for h in range(NH):
                    dve.wait_ge(ring_full, b * RING + i * 16 + (2 * NCH + 4 * u + 2 * k + h + 1) + 5)
                    xc = x_sb[:, h, bass.ds(i * (8 * T) + (2 * u + k) * T, T)]
                    v_.scalar_tensor_tensor(xc, ring[2 * k + h], DD[:, h:h + 1], xc, ALU.add, ALU.add)\
                        .then_inc(ring_used, 1)

            def final_pair(b, i, u):
                for k in range(2):
                    final(b, i, u, k)

            def b0_aggregate(b):
                dve.drain()
                for h in range(NH):
                    ins = v_.bn_aggr(mv[:, h, :], bn[:, h, :, :].rearrange("p c s -> p (c s)"))
                ins.then_inc(s0[0], 1)
                dve.drain()
                v_.tensor_scalar(NB, mv[:, :, 0], -1.0, None, ALU.mult)

            def b0_means(b):
                dve.wait_ge(s0[1], b + 1)
                v_.tensor_scalar(NM, ps_cg[:, 0:NH], -1.0, None, ALU.mult).then_inc(s0[6], 1)
                v_.tensor_tensor(DEV, mv[:, :, 0], ps_cg[:, 0:NH], ALU.subtract)
                dve.drain()
                v_.tensor_tensor(D2, DEV, DEV, ALU.mult)
                dve.drain()
                v_.tensor_tensor(SVAR, mv[:, :, 1], D2, ALU.add).then_inc(s0[2], 1)

            def b0_variances(b):
                dve.wait_ge(s0[3], b + 1)
                v_.tensor_scalar(S1, ps_cg[:, 8:8 + NH], EPS, None, ALU.add).then_inc(s0[4], 1)

            def b0_weights(b):
                dve.wait_ge(wh_ready, b + 1)
                for h in range(NH):
                    ins = v_.scalar_tensor_tensor(wqvk[:, 1, h, :], wqT[:, h, :], RR[:, h:h + 1],
                                                  wqvk[:, 0, h, :].bitcast(F32), ALU.mult, ALU.subtract)
                ins.then_inc(s0[7], 1)

            def b0_low(b, u):
                for h in range(NH):
                    low(b * NCH + u, u * T, u, h)

            def image(b, last):
                c0 = b * NCH
                v_.memset(acc[:, :], 0.0)
                v_.memset(gram[:, :], 0.0)
                v_.memset(negmax[:, 1:2], BIG)
                maximum_k(c0, 0)

                def stage_stats(i, h):
                    dve.wait_ge(stage_in[h], b * (NPR * 16) + i * 16 + 16)
                    v_.bn_stats(bn[:, h, bass.ds(i + NPR, 1), :].rearrange("p a s -> p (a s)"), stage[:, h, :])\
                        .then_inc(stage_used, 1)

                def step(c, i, u, low_next=True, k_next=True, sum_last=True):
                    g = c0 + c
                    maximum_q(g, u)
                    if low_next:
                        low(g + 2, (c + 2) * T, u, 0)
                    sums(g, u)
                    if sum_last:
                        accumulate(g - 1, 1 - u)
                    if k_next:
                        maximum_k(g + 1, 1 - u)
                    if low_next:
                        low(g + 2, (c + 2) * T, u, 1)
                    if not last:
                        stage_stats(i, u)

                step(0, 0, 0, sum_last=False)
                with dve.Fori(0, NPR - 2) as i:
                    for u in range(2):
                        step(i * 2 + u + 1, i + u, 1 - u)
                step(NCH - 3, NPR - 2, 1)
                step(NCH - 2, NPR - 1, 0, low_next=False)
                step(NCH - 1, NPR - 1, 1, low_next=False, k_next=False)
                dve.drain()
                dve.wait_ge(ctx_end, b + 1)
                v_.scalar_tensor_tensor(acc[:, :], acc[:, :], alpha[:, 1:2], ps_cg[:, 2 * HID:2 * HID + G1],
                                        ALU.mult, ALU.add)
                dve.drain()
                v_.reciprocal(DEV[:, 0:1], acc[:, HID:G1])
                dve.drain()
                v_.scalar_tensor_tensor(ctxm[:, :], acc[:, 0:HID], DEV[:, 0:1], headmask[:, :], ALU.mult, ALU.mult)\
                    .then_inc(s1[0], 1)
                dve.wait_ge(w_in[3], 80)
                dve.wait_ge(qT_sb, c0 + NCH + 1)
                v_.tensor_reduce(mu[:, 0:1], qs[:, :], axis=AXX, op=ALU.add)
                dve.drain()
                v_.tensor_scalar(mu[:, 1:2], mu[:, 0:1], 1.0 / N, None, ALU.mult)
                dve.wait_ge(cg_ready, c0 + (NCH + 1) + 1)
                v_.tensor_tensor(gram[:, :], gram[:, :], ps_cg[:, 0:2 * HID], ALU.add).then_inc(cg_used, 1)
                dve.drain()
                v_.scalar_tensor_tensor(gram_q[:, :], gram[:, HID:2 * HID], 2.0, gram[:, 0:HID], ALU.mult, ALU.add)\
                    .then_inc(s1[8], 1)
                dve.wait_ge(s1[3], b + 1)
                v_.tensor_copy(DELTA, ps_qT[:, C:C + NH])
                v_.scalar_tensor_tensor(pz[:, :], ps_qT[:, 0:C], 1.0 / N, MT[:, :], ALU.mult, ALU.mult)\
                    .then_inc(s1[4], 1)
                dve.drain()
                v_.tensor_tensor(D2, DELTA, DELTA, ALU.mult)
                v_.tensor_tensor(TT, vecs[:, 0, :], DELTA, ALU.add)
                dve.drain()
                dve.wait_ge(s1[5], b + 1)
                v_.tensor_tensor(VAR1, ps_qT[:, C + 4:C + 4 + NH], D2, ALU.subtract)
                dve.drain()
                v_.tensor_scalar(VB, VAR1, 0.0, EPS, ALU.max, ALU.add).then_inc(s1[6], 1)
                v_.tensor_tensor(TT, vecs[:, 0, :], TT, ALU.subtract)
                dve.wait_ge(s1[7], b + 1)
                v_.tensor_tensor(A, RS, vecs[:, 1, :], ALU.mult)
                dve.drain()
                v_.tensor_tensor(AD, A, DELTA, ALU.mult)
                v_.tensor_tensor(CC, TT, A, ALU.mult)
                dve.drain()
                v_.tensor_tensor(MEAN1, mv[:, :, 0], AD, ALU.add)
                v_.tensor_tensor(CC, CC, vecs[:, 2, :], ALU.add)
                dve.drain()
                v_.tensor_tensor(MEAN1, MEAN1, CC, ALU.add)
                v_.tensor_tensor(D2, AD, AD, ALU.mult)
                with dve.Fori(0, NPR) as i:
                    for u in range(2):
                        for h in range(NH):
                            n = 2 * u + h
                            dve.wait_ge(ring_full, b * RING + i * 4 + n + 6)
                            xc = x_sb[:, h, bass.ds(i * (2 * T) + u * T, T)]
                            v_.scalar_tensor_tensor(xc, ring[n], A[:, h:h + 1], xc, ALU.mult, ALU.add)\
                                .then_inc(ring_used, 1)
                dve.drain()
                dve.wait_ge(s1[6], b + 1)
                ins = v_.tensor_copy(TT, MEAN1)
                ins.then_inc(s2[0], 1)
                dve.wait_ge(sq_done, (b + 1) * (2 * NCH) + 1)
                v_.tensor_reduce(SQS, sq[:, :, :], axis=AXX, op=ALU.add)
                dve.drain()
                v_.scalar_tensor_tensor(VAR1, SQS, 1.0 / N, D2, ALU.mult, ALU.subtract)
                dve.wait_ge(s2[1], b + 1)
                v_.tensor_tensor(DEV1, MEAN1, ps_cg[:, 0:NH], ALU.subtract)
                v_.tensor_tensor(VEC, CC, ps_cg[:, 0:NH], ALU.subtract)
                dve.drain()
                v_.tensor_tensor(D2, DEV1, DEV1, ALU.mult)
                dve.drain()
                v_.tensor_tensor(SVAR, VAR1, D2, ALU.add).then_inc(s2[2], 1)
                dve.wait_ge(s2[3], b + 1)
                v_.tensor_scalar(S1, ps_cg[:, 8:8 + NH], EPS, None, ALU.add).then_inc(s2[4], 1)
                dve.wait_ge(s2[5], b + 1)
                v_.tensor_tensor(POOL, DEV1, R1, ALU.mult)
                v_.tensor_tensor(VEC, VEC, R1, ALU.mult)
                dve.drain()
                for h in range(NH):
                    ins = v_.tensor_scalar(pooled[:, h, :], ones[:, :], POOL[:, h:h + 1], None, ALU.mult)
                ins.then_inc(s2[6], 1)
                dve.wait_ge(s2[8], b + 1)
                v_.tensor_scalar(hid[:, 1, :], hid[:, 0, :], 1.0, None, ALU.add)
                dve.drain()
                v_.reciprocal(hid[:, 2, :], hid[:, 1, :])
                dve.drain()
                v_.tensor_tensor(hid[:, 3, :], ps_qT[:, 8:8 + J], hid[:, 2, :], ALU.mult).then_inc(hid_ready, 1)
                dve.drain()
                for h in range(NH):
                    dve.wait_ge(se_in[h], (b + 1) * 32)
                for j in range(JD):
                    for h in range(NH):
                        if j > 0:
                            dve.wait_ge(wb_step, b * (2 * JD) + 2 * j + h - 1)
                        v_.scalar_tensor_tensor(WB[:, h, :], se_sb[h].rearrange("p (o j) -> p o j", j=J)[:, :, j],
                                                hid[:, 3, j:j + 1], w1T[:, h, :] if j == 0 else WB[:, h, :],
                                                ALU.mult, ALU.add).then_inc(wb_step, 1)
                dve.drain()
                dve.wait_ge(prod_used, (b + 1) * (JP - 1))
                v_.tensor_tensor(WB[:, :, :].rearrange("p h o -> p (h o)"), WB[:, :, :].rearrange("p h o -> p (h o)"),
                                 wsum, ALU.add)
                dve.drain()
                for h in range(NH):
                    v_.tensor_scalar(WS[:, 0, h, :], WB[:, h, :], R1[:, h:h + 1], None, ALU.mult)
                dve.drain()
                for h in range(NH):
                    ins = v_.scalar_tensor_tensor(WS[:, 1, h, :], WB[:, h, :], R1[:, h:h + 1],
                                                  WS[:, 0, h, :].bitcast(F32), ALU.mult, ALU.subtract)
                ins.then_inc(s2[9], 1)
                dve.wait_ge(s2[10], b + 1)
                v_.tensor_tensor(DD, CC, ps_cg[:, 16:16 + NH], ALU.add)
                dve.drain()
                if last:
                    with dve.Fori(0, NQ) as i:
                        for u in range(4):
                            final_pair(b, i, u)
                    return
                for u in range(4):
                    final_pair(b, 0, u)
                with dve.Fori(0, NQ // 2) as i:
                    for u in range(4):
                        final_pair(b, i + 1, u)
                        stats(b + 1, i, u)
                b0_aggregate(b + 1)
                final_pair(b, NQ - 1, 0)
                b0_means(b + 1)
                final_pair(b, NQ - 1, 1)
                b0_variances(b + 1)
                final_pair(b, NQ - 1, 2)
                b0_weights(b + 1)
                final(b, NQ - 1, 3, 0)
                b0_low(b + 1, 0)
                final(b, NQ - 1, 3, 1)
                b0_low(b + 1, 1)

            with dve.Fori(0, NQ) as i:
                for u in range(4):
                    stats(0, i, u)
            b0_aggregate(0)
            b0_means(0)
            b0_variances(0)
            b0_weights(0)
            for u in range(2):
                b0_low(0, u)
            with dve.Fori(0, B - 1) as b:
                image(b, False)
            image(B - 1, True)


_INS = ["x", "L0_conv_qkv_w", "L0_conv_conv_w", "L0_conv_conv_b", "L0_conv_gamma", "L0_conv_beta",
        "L1_conv_w_conv", "L1_conv_w_se1", "L1_conv_w_se_out"]


def kernel(**inputs):
    import numpy as _np
    import concourse.bacc as _bacc
    from concourse import mybir as _mybir
    from concourse.bass_utils import run_bass_kernel_spmd as _run

    nc = _bacc.Bacc("TRN2", target_bir_lowering=False, num_devices=1)
    arrays, args = {}, []
    for name in _INS:
        a = _np.ascontiguousarray(inputs[name])
        arrays[f"in_{name}"] = a
        args.append(nc.dram_tensor(f"in_{name}", a.shape, _mybir.dt.from_np(a.dtype), kind="ExternalInput").ap())
    shape = arrays["in_x"].shape
    args.append(nc.dram_tensor("out_x2", shape, _mybir.dt.float32, kind="ExternalOutput").ap())
    block_program(nc, *args)
    r = _run(nc, [arrays], core_ids=[0])
    return r.results[0]["out_x2"]
```

```python
import concourse.bass as bass
from concourse import mybir
from contextlib import ExitStack

F32 = mybir.dt.float32
F32R = mybir.dt.float32r
ALU = mybir.AluOpType
ACT = mybir.ActivationFunctionType
AXX = mybir.AxisListType.X

P = 128
HEADS, DH = 4, 32
HID = HEADS * DH
GC = 8
T = 512
NT = T // P
EPS = 1e-5
BIG = 3.0e38


def block_program(nc, x, qkv_w, conv_w, conv_b, gamma, beta, w_conv, w_se1, w_se_out, out):
    B, C, H, W = x.shape
    N = H * W
    NH = C // P
    NCH = N // T
    NPR = NCH // 2
    NQ = NPR // 4
    J = w_se1.shape[0]
    G1 = HID + 1

    x_v = x.rearrange("b (h p) r w -> b p h (r w)", p=P)
    out_v = out.rearrange("b (h p) r w -> b p h (r w)", p=P)
    q_dram = nc.dram_tensor("q_dram", (B, P, N), F32, kind="Internal").ap()
    se_dram = nc.dram_tensor("se_dram", (NH, P, C * J), F32, kind="Internal").ap()

    ctx = ExitStack()
    with ctx:
        def sb(name, shape, dtype=F32):
            return ctx.enter_context(nc.sbuf_tensor(name, shape, dtype))

        def sem(name):
            return ctx.enter_context(nc.semaphore(name))

        x_sb = sb("x_sb", [P, NH, N])
        ident = sb("ident", [P, P])
        ones = sb("ones", [P, P])
        group = sb("group", [P, P])
        headmask = sb("headmask", [P, P])
        powers = sb("powers", [P, NH])
        wqT = sb("wqT", [P, NH, 3 * HID])
        wqvk = sb("wqvk", [P, 2, NH, 3 * HID], F32R)
        convT = sb("convT", [P, C])
        w1T = sb("w1T", [P, NH, C])
        se1T = sb("se1T", [P, NH, J])
        vecs = sb("vecs", [P, 3, NH])
        work = sb("work", [P, 8 * T])
        e_k = work[:, 0:2 * T].rearrange("p (u n) -> p u n", u=2)
        q_sb = work[:, 2 * T:4 * T].rearrange("p (u a d) -> p u a d", u=2, d=DH)
        qT = work[:, 4 * T:6 * T].rearrange("p (u n) -> p u n", u=2)
        e_kT = work[:, 6 * T:7 * T].rearrange("p (t c) -> p t c", t=NT)
        q_tok = work[:, 2 * T:4 * T].rearrange("p (u t c) -> p u t c", u=2, t=NT)
        xhl = sb("xhl", [P, 2, 2, NH, T], F32R)
        qhl = sb("qhl", [P, 2, NT, 2, HID], F32R)
        v_sb = sb("v_sb", [P, 2, NT, G1])
        qm = sb("qm", [P, NT * HEADS])
        qsum = sb("qsum", [P, NT * HEADS])
        qinv = sb("qinv", [P, 2, NT * HEADS])
        negk = sb("negk", [P, 1])
        negmax = sb("negmax", [P, 2])
        alpha = sb("alpha", [P, 2])
        acc = sb("acc", [P, G1])
        gram = sb("gram", [P, 2 * HID])
        gram_q = sb("gram_q", [P, HID])
        qs = sb("qs", [P, NCH])
        mu = sb("mu", [P, 2])
        bn = sb("bn", [P, NH, NCH, 6])
        mv = sb("mv", [P, NH, 2])
        sm = sb("sm", [P, 21, NH])
        MT = sb("MT", [P, C])
        ctxm = sb("ctxm", [P, P])
        hid = sb("hid", [P, 4, J])
        sq = sb("sq", [P, NH, NCH])
        WB = sb("WB", [P, NH, C])
        WS = sb("WS", [P, 2, NH, C], F32R)
        ql = sb("ql", [P, 4, T])
        (DEV, SVAR, RR, NB, DELTA, D2, VB, RS, A, TT, CC, SQS, AD, MEAN1, VAR1, DEV1, S1, R1,
         VEC, DD, NM) = (sm[:, n, :] for n in range(21))
        se_sb = [xhl[:, :, :, :, :].rearrange("p u s h n -> p (u s h n)").bitcast(F32), work[:, :]]
        stage = ql[:, 2:4, :]
        prod = [ql[:, n, :] for n in range(3)]
        wsum = ql[:, 3, :]
        x1_first = qhl[:, :, :, :, :].rearrange("p u t s c -> p (u t s c)").rearrange("p (s h n) -> p s h n", s=2, h=NH)
        se1R = sb("se1R", [P, NH, J])
        diag = [v_sb[:, n // NT, n % NT, 0:P] for n in range(2 * NT)]
        pz = sb("pz", [P, C])
        pooled = pz[:, :].rearrange("p (h c) -> p h c", h=NH)
        wq_raw = work[:, 0:3 * C].rearrange("p (t c) -> p t c", t=3)
        cw_raw = work[:, 3 * C:4 * C].rearrange("p (t c) -> p t c", t=NH)
        w1_raw = work[:, 4 * C:6 * C].rearrange("p (t c) -> p t c", t=NH)

        PS = ctx.enter_context(nc.psum_tensor("PS", [P, 8, T], F32))
        ps_k = PS[:, 0, :]
        ps_qv = [PS[:, 1 + 2 * u:3 + 2 * u, :].rearrange("p a (b c) -> p (a b) c", c=2 * HID)
                 for u in range(2)]
        ps_eT, ps_qT, ps_cg = PS[:, 5, :], PS[:, 6, :], PS[:, 7, :]
        ring = [PS[:, 1 + n, :] for n in range(4)]
        ps_wb = [PS[:, 0, 0:C], PS[:, 5, 0:C]]

        w_in = [sem(f"w_in{n}") for n in range(4)]
        se_out = [sem(f"se_out{n}") for n in range(NH)]
        se_in = [sem(f"se_in{n}") for n in range(NH)]
        pool_step, consts = sem("pool_step"), sem("consts")
        w_tr, w_cp = sem("w_tr"), sem("w_cp")
        x_in = [sem(f"x_in{n}") for n in range(4)]
        out_st = [sem(f"out_st{n}") for n in range(4)]
        q_st = [sem(f"q_st{n}") for n in range(2)]
        q_in = [sem(f"q_in{n}") for n in range(4)]
        stage_in = [sem(f"stage_in{n}") for n in range(NH)]
        stage_used = sem("stage_used")
        sp_passed = sem("sp_passed")
        xh_ready, xl_ready = sem("xh_ready"), sem("xl_ready")
        k_ready, qv_ready = sem("k_ready"), sem("qv_ready")
        negmax_ready, ek_ready, alpha_ready = sem("negmax_ready"), sem("ek_ready"), sem("alpha_ready")
        q_shift, q_exp, q_inv, qn_ready = sem("q_shift"), sem("q_exp"), sem("q_inv"), sem("qn_ready")
        v_ready, eT_ps, eT_sb = sem("v_ready"), sem("eT_ps"), sem("eT_sb")
        qh_ready, ql_ready = sem("qh_ready"), sem("ql_ready")
        qT_ps, qT_sb, cg_ready, cg_used = sem("qT_ps"), sem("qT_sb"), sem("cg_ready"), sem("cg_used")
        x1h_ready, x1l_ready = sem("x1h_ready"), sem("x1l_ready")
        x1_used = sem("x1_used")
        ring_full, ring_used, sq_done = sem("ring_full"), sem("ring_used"), sem("sq_done")
        xstat_ready, xmean_ps, xvar_ready, xgvar_ps = (sem(n) for n in ("xstat_ready", "xmean_ps", "xvar_ready", "xgvar_ps"))
        xgvar_ready, xdev_ready, nm_ready, wl_ready = (sem(n) for n in ("xgvar_ready", "xdev_ready", "nm_ready", "wl_ready"))
        wh_ready = sem("wh_ready")
        ctxm_ready, mt_ps, mt_ready, gram_mt_ps = (sem(n) for n in ("ctxm_ready", "mt_ps", "mt_ready", "gram_mt_ps"))
        pz_ready, yvar_ps, yvar_ready, ydev_ready = (sem(n) for n in ("pz_ready", "yvar_ps", "yvar_ready", "ydev_ready"))
        gram_ready, ctx_end, mu_ready = (sem(n) for n in ("gram_ready", "ctx_end", "mu_ready"))
        mean1_ready, gmean1_ps, var1_ready, gvar1_ps = (sem(n) for n in ("mean1_ready", "gmean1_ps", "var1_ready", "gvar1_ps"))
        gvar1_ready, dev1_ready, se1r_ready, hidden_ps = (sem(n) for n in ("gvar1_ready", "dev1_ready", "se1r_ready", "hidden_ps"))
        hidden_exp, const_ps, hid_ready, prod_ready = (sem(n) for n in ("hidden_exp", "const_ps", "hid_ready", "prod_ready"))
        prod_used, wb_step, diag_dve, diag_act = (sem(n) for n in ("prod_used", "wb_step", "diag_dve", "diag_act"))
        wb_ready, ws_ready = (sem(n) for n in ("wb_ready", "ws_ready"))

        block = ctx.enter_context(nc.Block())
        JP = 4
        JM = 5
        JD = J - JP - JM
        PARTS = ((0, 0), (0, 1), (1, 0))
        RING = 2 * 2 * NCH

        @block.sync
        def _(sp):
            for s in (*x_in, *out_st, *q_st, *se_out):
                sp.sem_inc(s, 16)
            sp.dma_start(wq_raw, qkv_w.rearrange("(t p) c -> p t c", p=P)).then_inc(w_in[0], 16)
            sp.dma_start(cw_raw, conv_w.rearrange("(t p) c -> p t c", p=P)).then_inc(w_in[1], 16)
            sp.dma_start(w1_raw, w_conv.rearrange("(t p) c i j -> p t (c i j)", p=P)).then_inc(w_in[2], 16)
            def load_pair(b, i, u):
                sp.dma_start(x_sb[:, :, bass.ds(i * (8 * T) + u * (2 * T), 2 * T)],
                             x_v[b, :, :, bass.ds(i * (8 * T) + u * (2 * T), 2 * T)]).then_inc(x_in[u], 16)

            with sp.Fori(0, NQ) as i:
                for u in range(4):
                    sp.wait_ge(x_in[u], i * 16 + 16)
                    load_pair(0, i, u)
            with nc.allow_non_contiguous_dma("vectors and the squeeze weights, once"):
                for n, v in enumerate((conv_b, gamma, beta)):
                    sp.dma_start(vecs[:, n, :], v.rearrange("(h p) -> p h", p=P)).then_inc(w_in[3], 16)
                    sp.wait_ge(w_in[3], 16 * (n + 1))
                for h in range(NH):
                    sp.dma_start(se1T[:, h, :], w_se1[:, h * P:(h + 1) * P].rearrange("j p -> p j")).then_inc(w_in[3], 16)
                    sp.wait_ge(w_in[3], 16 * (h + 4))

            def store_pair(b, i, u):
                sp.wait_ge(ring_used, b * RING + i * 16 + (2 * NCH + 4 * (u + 1)) + 4)
                sp.sem_inc(sp_passed, 1)
                sp.wait_ge(out_st[u], b * (NQ * 16) + i * 16 + 16)
                sp.sem_inc(sp_passed, 1)
                sp.dma_start(out_v[b, :, :, bass.ds(i * (8 * T) + u * (2 * T), 2 * T)],
                             x_sb[:, :, bass.ds(i * (8 * T) + u * (2 * T), 2 * T)]).then_inc(out_st[u], 16)

            def load_next(b, i, u):
                sp.wait_ge(out_st[u], b * (NQ * 16) + (i + 1) * 16 + 16)
                sp.sem_inc(sp_passed, 1)
                sp.wait_ge(x_in[u], b * (NQ * 16) + (i + NQ) * 16 + 16)
                sp.sem_inc(sp_passed, 1)
                load_pair(b + 1, i, u)

            def relay(i, h):
                rows = C // NPR
                sp.wait_ge(se_out[h], i * 16 + 16)
                sp.sem_inc(sp_passed, 1)
                with nc.allow_non_contiguous_dma("the squeeze weights, once"):
                    sp.dma_start(se_dram[h].rearrange("p (o j) -> p o j", j=J)[:, bass.ds(i * rows, rows), :],
                                 w_se_out.rearrange("(o h p) j -> h p o j", h=NH, p=P)[h][:, bass.ds(i * rows, rows), :])\
                      .then_inc(se_out[h], 16)

            def image(b, first, last):
                def spill(i, u):
                    sp.wait_ge(qT_sb, b * NCH + i * 2 + u + 2)
                    sp.sem_inc(sp_passed, 1)
                    sp.dma_start(q_dram[b, :, bass.ds(i * (2 * T) + u * T, T)], qT[:, u, :]).then_inc(q_st[u], 16)

                def load_stage(i, h):
                    sp.wait_ge(stage_used, b * NCH + i * 2 + (h - 1))
                    sp.sem_inc(sp_passed, 1)
                    sp.wait_ge(stage_in[h], b * (NPR * 16) + i * 16)
                    sp.sem_inc(sp_passed, 1)
                    sp.dma_start(stage[:, h, :], x_v[b + 1, :, h, bass.ds(i * T + N // 2, T)]).then_inc(stage_in[h], 16)

                with sp.Fori(0, NPR - 1) as i:
                    for u in range(2):
                        spill(i, u)
                        if not last:
                            load_stage(i + 1, u)
                        if first:
                            relay(i, u)
                if first:
                    for u in range(2):
                        relay(NPR - 1, u)

                def load_queries(i, n, first=False):
                    if not first:
                        sp.wait_ge(ring_full, b * RING + i * 8 + (2 * n - 1))
                        sp.sem_inc(sp_passed, 1)
                    sp.dma_start(ql[:, n, :], q_dram[b, :, bass.ds(i * (4 * T) + n * T, T)]).then_inc(q_in[n], 16)

                for u in range(2):
                    sp.wait_ge(q_st[u], b * (NPR * 16) + (NPR - 1) * 16 + 16)
                sp.sem_inc(sp_passed, 1)
                for n in range(2):
                    load_queries(0, n, True)
                if not last:
                    sp.wait_ge(stage_used, (b + 1) * NCH)
                    sp.sem_inc(sp_passed, 1)
                for n in range(2, 4):
                    load_queries(0, n, True)
                for u in range(2):
                    spill(NPR - 1, u)
                for u in range(2):
                    sp.wait_ge(q_st[u], (b + 1) * (NPR * 16) + 16)
                sp.sem_inc(sp_passed, 1)
                for i in range(1, 5):
                    for n in range(4):
                        load_queries(i, n)
                    if i == 1:
                        sp.wait_ge(ctxm_ready, b + 1)
                        sp.sem_inc(sp_passed, 1)
                    h, half = (i - 1) // 2, bass.ds((i - 1) % 2 * (C * J // 2), C * J // 2)
                    sp.wait_ge(se_out[h], NPR * 16 + 16)
                    sp.dma_start(se_sb[h][:, half], se_dram[h][:, half]).then_inc(se_in[h], 16)
                with sp.Fori(5, NCH // 4) as i:
                    for n in range(4):
                        load_queries(i, n)
                if last:
                    with sp.Fori(0, NQ) as i:
                        for u in range(4):
                            store_pair(b, i, u)
                    return
                for u in range(4):
                    store_pair(b, 0, u)
                    if u >= 1:
                        load_next(b, 0, u - 1)
                with sp.Fori(0, NQ - 1) as i:
                    for u in range(4):
                        store_pair(b, i + 1, u)
                        load_next(b, i + (u + 3) // 4, (u + 3) % 4)
                load_next(b, NQ - 1, 3)

            image(0, True, False)
            with sp.Fori(1, B - 1) as b:
                image(b, False, False)
            image(B - 1, False, True)
            for u in range(4):
                sp.wait_ge(out_st[u], B * NQ * 16 + 16)

        @block.gpsimd
        def _(pool):
            steps = [0]

            def step(ins):
                steps[0] += 1
                ins.then_inc(pool_step, 1)
                pool.wait_ge(pool_step, steps[0])

            step(nc.gpsimd.memset(ident[:, :], 0.0))
            step(nc.gpsimd.affine_select(out=ident[:, :], in_=ident[:, :], compare_op=ALU.not_equal, fill=1.0,
                                         base=0, pattern=[[-1, P]], channel_multiplier=1))
            step(nc.gpsimd.memset(ones[:, :], 1.0))
            step(nc.gpsimd.memset(powers[:, :], -0.5))
            step(nc.gpsimd.memset(v_sb[:, :, :, HID:G1], 1.0))
            for tile, size, value in ((group, GC, 1.0 / GC), (headmask, DH, float(DH) ** -0.5 / N)):
                step(nc.gpsimd.memset(tile[:, :], value))
                v = tile[:, :].rearrange("p (g s) -> p g s", s=size)
                step(nc.gpsimd.affine_select(out=v, in_=v, compare_op=ALU.is_ge, fill=0.0, base=0,
                                             pattern=[[-size, P // size], [0, size]], channel_multiplier=1))
                step(nc.gpsimd.affine_select(out=v, in_=v, compare_op=ALU.is_ge, fill=0.0, base=size - 1,
                                             pattern=[[size, P // size], [0, size]], channel_multiplier=-1))
            pool.sem_inc(consts, 1)

            def b0_deviation(b):
                pool.wait_ge(xgvar_ready, b + 1)
                nc.gpsimd.tensor_tensor(RR, S1, powers[:, :], ALU.pow).then_inc(xdev_ready, 1)

            def image(b, last):
                c0 = b * NCH

                def queries(g, u):
                    pool.wait_ge(q_inv, g + 1)
                    q4 = q_sb[:, u, :, :].rearrange("p (t e) d -> p t e d", e=HEADS)
                    nc.gpsimd.tensor_tensor(
                        q4, q4, qinv[:, u, :].rearrange("p (t e) -> p t e", e=HEADS)[:, :, :, None]
                        .to_broadcast([P, NT, HEADS, DH]), ALU.mult).then_inc(qn_ready, 1)
                    pool.wait_ge(qh_ready, g + 1)
                    nc.gpsimd.tensor_tensor(qhl[:, u, :, 1, :], q_tok[:, u, :, :], qhl[:, u, :, 0, :].bitcast(F32),
                                            ALU.subtract).then_inc(ql_ready, 1)

                with pool.Fori(0, NPR) as i:
                    for u in range(2):
                        queries(c0 + i * 2 + u, u)
                pool.wait_ge(yvar_ready, b + 1)
                nc.gpsimd.tensor_tensor(RS, VB, powers[:, :], ALU.pow).then_inc(ydev_ready, 1)
                for h in range(NH):
                    pool.wait_ge(x1h_ready, c0 * 2 + h + 1)
                    nc.gpsimd.tensor_tensor(x1_first[:, 1, h, :], x_sb[:, h, 0:T], x1_first[:, 0, h, :].bitcast(F32),
                                            ALU.subtract).then_inc(x1l_ready, 1)
                pool.wait_ge(gvar1_ready, b + 1)
                nc.gpsimd.tensor_tensor(R1, S1, powers[:, :], ALU.pow).then_inc(dev1_ready, 1)
                for k in range(1, JP):
                    pool.wait_ge(prod_ready, b * JP + k + 1)
                    if k >= 2:
                        pool.wait_ge(prod_used, b * (JP - 1) + k - 1)
                    nc.gpsimd.tensor_tensor(wsum, prod[0] if k == 1 else wsum, prod[k % 3], ALU.add)\
                      .then_inc(prod_used, 1)
                def low(i, chunks=(0, 1)):
                    for u in chunks:
                        for h in range(NH):
                            pool.wait_ge(x1h_ready, c0 * 2 + i * 4 + 2 * u + h + 1)
                            nc.gpsimd.tensor_tensor(xhl[:, u, 1, h, :], x_sb[:, h, bass.ds(i * (2 * T) + u * T, T)],
                                                    xhl[:, u, 0, h, :].bitcast(F32), ALU.subtract)\
                              .then_inc(x1l_ready, 1)

                low(0, (1,))
                if last:
                    with pool.Fori(1, NPR) as i:
                        low(i)
                    return
                with pool.Fori(1, NPR - 1) as i:
                    low(i)
                b0_deviation(b + 1)
                low(NPR - 1)

            b0_deviation(0)
            with pool.Fori(0, B - 1) as b:
                image(b, False)
            image(B - 1, True)

        @block.scalar
        def _(act):
            def high(g, c, u):
                act.wait_ge(qv_ready, g + 1)
                for h in range(NH):
                    nc.scalar.activation(xhl[:, u, 0, h, :], x_sb[:, h, bass.ds(c, T)], ACT.Identity,
                                         bias=NM[:, h:h + 1]).then_inc(xh_ready, 1)

            def exp_k(b, g, u):
                act.wait_ge(negmax_ready, g + 1)
                act.wait_ge(eT_ps, g + 1)
                nc.scalar.activation(e_k[:, u, :], ps_k, ACT.Exp, bias=negmax[:, u:u + 1]).then_inc(ek_ready, 1)
                act.wait_ge(cg_used, g + 1)
                nc.scalar.activation(alpha[:, u:u + 1], negmax[:, 1 - u:2 - u], ACT.Exp, scale=-1.0,
                                     bias=negmax[:, u:u + 1]).then_inc(alpha_ready, 1)

            def copy_v(g, u):
                act.wait_ge(q_shift, g + 2)
                act.wait_ge(cg_ready, g + 1)
                nc.scalar.activation(v_sb[:, u, :, 0:HID], ps_qv[u][:, :, HID:2 * HID], ACT.Copy).then_inc(v_ready, 1)

            def exp_q(g, u):
                act.wait_ge(q_shift, g + 2)
                nc.scalar.activation(q_sb[:, u, :, :], q_sb[:, u, :, :], ACT.Exp).then_inc(q_exp, 1)

            def copy_eT(g):
                act.wait_ge(eT_ps, g + 3)
                act.wait_ge(cg_ready, g + 2)
                nc.scalar.activation(e_kT[:, :, :], ps_eT.rearrange("p (t c) -> p t c", t=NT), ACT.Copy)\
                  .then_inc(eT_sb, 1)

            def high_q(g, u):
                act.wait_ge(qn_ready, g + 1)
                nc.scalar.activation(qhl[:, u, :, 0, :], q_tok[:, u, :, :], ACT.Copy).then_inc(qh_ready, 1)

            def copy_qT(g, c, u, spilled):
                act.wait_ge(qT_ps, g + 1)
                act.wait_ge(q_st[u], spilled + 16)
                nc.scalar.activation(qT[:, u, :], ps_qT, ACT.Copy,
                                     accum_out=qs[:, bass.ds(c, 1)]).then_inc(qT_sb, 1)

            def b0_weights(b):
                act.wait_ge(xdev_ready, b + 1)
                for h in range(NH):
                    ins = nc.scalar.activation(wqvk[:, 0, h, :], wqT[:, h, :], ACT.Copy, scale=RR[:, h:h + 1])
                ins.then_inc(wh_ready, 1)

            def b0_high(b):
                act.wait_ge(nm_ready, b + 1)
                for u in range(2):
                    act.wait_ge(ring_full, b * RING + 2 * u + 3)
                    high(b * NCH + u, u * T, u)

            def image(b, first, last):
                c0 = b * NCH
                st0 = b * (NPR * 16)
                if not last:
                    for h in range(NH):
                        if not first:
                            act.wait_ge(stage_in[h], b * (NPR * 16))
                        act.dma_start(stage[:, h, :], x_v[b + 1, :, h, N // 2:N // 2 + T]).then_inc(stage_in[h], 16)
                exp_k(b, c0, 0)

                def step(c, u, spilled, high_next=True, k_next=True, qT_last=True):
                    g = c0 + c
                    if high_next:
                        high(g + 2, (c + 2) * T, u)
                    exp_q(g, u)
                    copy_v(g, u)
                    if not k_next:
                        copy_eT(g)
                    if qT_last:
                        copy_qT(g - 1, c - 1, 1 - u, spilled)
                    if k_next:
                        copy_eT(g)
                    if k_next:
                        exp_k(b, g + 1, 1 - u)
                    high_q(g, u)

                step(0, 0, 0, qT_last=False)
                with act.Fori(0, NPR // 2 - 2) as i:
                    step(i * 2 + 1, 1, st0 + i * 16)
                    step(i * 2 + 2, 0, st0 + i * 16)
                for n in range(4):
                    act.wait_ge(x_in[n], (b + 1) * (NQ * 16) + 16)
                with act.Fori(NPR // 2 - 2, NPR - 2) as i:
                    step(i * 2 + 1, 1, st0 + i * 16)
                    step(i * 2 + 2, 0, st0 + i * 16)
                step(NCH - 3, 1, st0 + (NPR - 2) * 16)
                step(NCH - 2, 0, st0 + (NPR - 2) * 16, high_next=False)
                step(NCH - 1, 1, st0 + (NPR - 1) * 16, high_next=False, k_next=False)
                act.wait_ge(mt_ps, b + 1)
                nc.scalar.activation(MT[:, :], ps_eT[:, 0:C], ACT.Copy).then_inc(mt_ready, 1)
                copy_qT(c0 + (NCH - 1), NCH - 1, 1, st0 + (NPR - 1) * 16)
                act.wait_ge(yvar_ready, b + 1)
                def squares(i):
                    for u in range(2):
                        for h in range(NH):
                            n = i * 4 + 2 * u + h
                            act.wait_ge(ring_used, b * RING + n + 5)
                            act.wait_ge(sq_done, b * (2 * NCH) + n + 1)
                            nc.scalar.activation((ps_k, ps_eT)[h], x_sb[:, h, bass.ds(i * (2 * T) + u * T, T)],
                                                 ACT.Square, bias=NB[:, h:h + 1],
                                                 accum_out=sq[:, h, bass.ds(i * 2 + u, 1)]).then_inc(sq_done, 1)

                with act.Fori(0, NPR - 2) as i:
                    squares(i)
                for h in range(NH):
                    nc.scalar.activation(x1_first[:, 0, h, :], x_sb[:, h, 0:T], ACT.Copy).then_inc(x1h_ready, 1)
                for i in range(NPR - 2, NPR):
                    squares(i)
                act.wait_ge(hidden_ps, b + 1)
                nc.scalar.activation(hid[:, 0, :], ps_qT[:, 8:8 + J], ACT.Exp, scale=-1.0).then_inc(hidden_exp, 1)
                act.wait_ge(hid_ready, b + 1)
                for h in range(NH):
                    act.wait_ge(se_in[h], (b + 1) * 32)
                def diagonals(ns):
                    for n in ns:
                        j = JD + JP + n
                        nc.scalar.activation(diag[n], ident[:, :], ACT.Copy, scale=hid[:, 3, j:j + 1])\
                          .then_inc(diag_act, 1)

                for k in range(JP):
                    if k >= 3:
                        act.wait_ge(prod_used, b * (JP - 1) + k - 2)
                    for h in range(NH):
                        ins = nc.scalar.activation(prod[k % 3][:, h * C:(h + 1) * C],
                                                   se_sb[h].rearrange("p (o j) -> p o j", j=J)[:, :, JD + k],
                                                   ACT.Copy, scale=hid[:, 3, JD + k:JD + k + 1])
                    ins.then_inc(prod_ready, 1)
                    if k == 1:
                        diagonals(range(2, JM))
                def high_x1(i, chunks=(0, 1)):
                    for u in chunks:
                        for h in range(NH):
                            if h == 0:
                                act.wait_ge(x1_used, c0 + i * 2 + u + 1)
                            else:
                                act.wait_ge(ring_full, b * RING + (2 * NCH) + i * 4 + 2 * u + 3)
                            nc.scalar.activation(xhl[:, u, 0, h, :], x_sb[:, h, bass.ds(i * (2 * T) + u * T, T)],
                                                 ACT.Copy).then_inc(x1h_ready, 1)

                act.wait_ge(ws_ready, b * NH + 1)
                high_x1(0, (1,))
                if last:
                    with act.Fori(1, NPR) as i:
                        high_x1(i)
                    return
                with act.Fori(1, NPR - 1) as i:
                    high_x1(i)
                b0_weights(b + 1)
                high_x1(NPR - 1)
                b0_high(b + 1)

            b0_weights(0)
            b0_high(0)
            image(0, True, False)
            with act.Fori(1, B - 1) as b:
                image(b, False, False)
            image(B - 1, False, True)

        @block.tensor
        def _(pe):
            mm = nc.tensor.matmul
            pe.wait_ge(consts, 1)
            for n in range(3):
                pe.wait_ge(w_in[n], 16)
            tr = 0
            for raw_w, blocks in ((wq_raw, 3), (cw_raw, 1), (w1_raw, 2)):
                for h in range(NH):
                    if raw_w is cw_raw:
                        srcs = [cw_raw[:, h, :]]
                    else:
                        srcs = [raw_w[:, t, h * P:(h + 1) * P] for t in range(blocks)]
                    if tr >= 2:
                        pe.wait_ge(w_cp, tr - 1)
                    for t, s in enumerate(srcs):
                        last = nc.tensor.transpose(PS[:, tr % 2, t * P:(t + 1) * P], s, ident[:, :])
                    last.then_inc(w_tr, 1)
                    tr += 1
            pe.wait_ge(w_cp, 6)
            pe.sem_inc(cg_ready, 2)
            pe.sem_inc(eT_ps, 2)
            pe.sem_inc(ring_full, 5)
            pe.sem_inc(x1_used, 2)

            def product_k(g, u):
                pe.wait_ge(xl_ready, g + 1)
                pe.wait_ge(ek_ready, g + 1)
                n = 0
                for h in range(NH):
                    for a, b in PARTS:
                        last = mm(ps_k, wqvk[:, a, h, 2 * HID:3 * HID], xhl[:, u, b, h, :],
                                  start=(n == 0), stop=(n == len(PARTS) * NH - 1))
                        n += 1
                last.then_inc(k_ready, 1)

            def product_qv(g, u):
                pe.wait_ge(v_ready, g + 1)
                for t in range(NT):
                    n = 0
                    for h in range(NH):
                        for a, b in PARTS:
                            last = mm(ps_qv[u][:, t, :], xhl[:, u, a, h, t * P:(t + 1) * P], wqvk[:, b, h, 0:2 * HID],
                                      start=(n == 0), stop=(n == len(PARTS) * NH - 1))
                            n += 1
                last.then_inc(qv_ready, 1)

            def transpose_k(g, u):
                pe.wait_ge(ek_ready, g + 2)
                pe.wait_ge(eT_sb, g + 1)
                for t in range(NT):
                    last = nc.tensor.transpose(ps_eT[:, t * P:(t + 1) * P], e_k[:, u, t * P:(t + 1) * P], ident[:, :])
                last.then_inc(eT_ps, 1)

            def context(g, u):
                pe.wait_ge(cg_used, g + 2)
                pe.wait_ge(eT_sb, g + 2)
                pe.wait_ge(v_ready, g + 3)
                for t in range(NT):
                    last = mm(ps_cg[:, 2 * HID:2 * HID + G1], e_kT[:, t, :], v_sb[:, u, t, :],
                              start=(t == 0), stop=(t == NT - 1))
                return last

            def transpose_q(g, u):
                pe.wait_ge(qn_ready, g + 1)
                pe.wait_ge(qT_sb, g + 1)
                for t in range(NT):
                    last = nc.tensor.transpose(ps_qT[:, t * P:(t + 1) * P], q_tok[:, u, t, :], ident[:, :])
                last.then_inc(qT_ps, 1)

            def gram_matrix(g, u):
                pe.wait_ge(ql_ready, g + 1)
                for t in range(NT):
                    last = mm(ps_cg[:, 0:2 * HID], qhl[:, u, t, 0, :], qhl[:, u, t, :, :].rearrange("p s c -> p (s c)"),
                              start=(t == 0), stop=(t == NT - 1))
                last.then_inc(cg_ready, 1)

            def step(g, u, gram=True):
                product_k(g, u)
                if gram:
                    gram_matrix(g - 2, u)
                transpose_k(g - 1, 1 - u)
                product_qv(g, u)
                context(g - 1, 1 - u)
                transpose_q(g - 1, 1 - u)

            def mixed(b, i, n, h):
                pe.wait_ge(ring_used, b * RING + i * 8 + 2 * n + h + 1)
                mm(ring[n % 2 * 2 + h], MT[:, h * P:(h + 1) * P], ql[:, n, :],
                   start=True, stop=True).then_inc(ring_full, 1)

            def b0_means(b):
                pe.wait_ge(xstat_ready, b + 1)
                mm(ps_cg[:, 0:NH], group[:, :], mv[:, :, 0], start=True, stop=True).then_inc(xmean_ps, 1)

            def b0_variances(b):
                pe.wait_ge(xvar_ready, b + 1)
                mm(ps_cg[:, 8:8 + NH], group[:, :], SVAR, start=True, stop=True).then_inc(xgvar_ps, 1)

            def image(b, last):
                c0 = b * NCH
                pe.wait_ge(wl_ready, b + 1)
                product_k(c0, 0)
                pe.wait_ge(ring_used, b * RING + 4)
                product_qv(c0, 0)
                step(c0 + 1, 1, gram=False)
                with pe.Fori(1, NPR) as i:
                    for u in range(2):
                        step(c0 + i * 2 + u, u)
                gram_matrix(c0 + (NCH - 2), 0)
                transpose_k(c0 + (NCH - 1), 1)
                context(c0 + (NCH - 1), 1).then_inc(ctx_end, 1)
                pe.wait_ge(ctxm_ready, b + 1)
                mm(ps_eT[:, 0:C], ctxm[:, :], convT[:, :], start=True, stop=True).then_inc(mt_ps, 1)
                transpose_q(c0 + (NCH - 1), 1)
                gram_matrix(c0 + (NCH - 1), 1)
                for n in range(2):
                    pe.wait_ge(q_in[n], b * (NCH * 4) + 16)
                pe.wait_ge(mt_ready, b + 1)
                mixed(b, 0, 0, 0)
                pe.wait_ge(gram_ready, b + 1)
                mm(ps_k[:, 0:C], gram_q[:, :], MT[:, :], start=True, stop=True)
                pe.wait_ge(mu_ready, b + 1)
                for h in range(NH):
                    ins = mm(ps_qT[:, C + h:C + h + 1], MT[:, h * P:(h + 1) * P], mu[:, 1:2], start=True, stop=True)
                ins.then_inc(gram_mt_ps, 1)
                mixed(b, 0, 0, 1)
                pe.wait_ge(pz_ready, b + 1)
                for h in range(NH):
                    ins = mm(ps_qT[:, C + 4 + h:C + 5 + h], pz[:, h * P:(h + 1) * P], ones[:, 0:1], start=True, stop=True)
                ins.then_inc(yvar_ps, 1)
                for h in range(NH):
                    mixed(b, 0, 1, h)

                def mixed_chunk(i, n):
                    pe.wait_ge(q_in[n], b * (NCH * 4) + i * 16 + 16)
                    for h in range(NH):
                        mixed(b, i, n, h)

                for n in range(2, 4):
                    mixed_chunk(0, n)
                pe.wait_ge(mean1_ready, b + 1)
                mm(ps_cg[:, 0:NH], group[:, :], MEAN1, start=True, stop=True).then_inc(gmean1_ps, 1)
                with pe.Fori(1, NCH // 4) as i:
                    for n in range(4):
                        mixed_chunk(i, n)
                pe.wait_ge(var1_ready, b + 1)
                mm(ps_cg[:, 8:8 + NH], group[:, :], SVAR, start=True, stop=True).then_inc(gvar1_ps, 1)
                pe.wait_ge(se1r_ready, b + 1)
                for h in range(NH):
                    ins = mm(ps_qT[:, 8:8 + J], pooled[:, h, :], se1R[:, h, :], start=(h == 0), stop=(h == NH - 1))
                ins.then_inc(hidden_ps, 1)
                for h in range(NH):
                    pe.wait_ge(se_in[h], (b + 1) * 32)
                for n in range(JM):
                    if n < 2:
                        pe.wait_ge(diag_dve, b * 2 + n + 1)
                    else:
                        pe.wait_ge(diag_act, b * (JM - 2) + n - 1)
                    for h in range(NH):
                        ins = mm(ps_wb[h], diag[n], se_sb[h].rearrange("p (o j) -> p o j", j=J)[:, :, JD + JP + n],
                                 start=(n == 0), stop=(n == JM - 1))
                ins.then_inc(wb_ready, 1)

                def output_constants():
                    for o in range(NH):
                        for h in range(NH):
                            ins = mm(ps_cg[:, 16 + o:17 + o], WB[:, h, o * P:(o + 1) * P], VEC[:, h:h + 1],
                                     start=(h == 0), stop=(h == NH - 1))
                    ins.then_inc(const_ps, 1)

                def final_pair(i, first=False):
                    for u in range(2):
                        parts = x1_first if first and u == 0 else xhl[:, u, :, :, :]
                        for o in range(NH):
                            pe.wait_ge(ring_used, b * RING + (2 * NCH) + i * 4 + 2 * u + o + 1)
                        for h in range(NH):
                            if first and u == 0:
                                pe.wait_ge(ws_ready, b * NH + h + 1)
                            pe.wait_ge(x1l_ready, c0 * 2 + i * 4 + 2 * u + h + 1)
                            for o in range(NH):
                                for m, (a, c) in enumerate(PARTS):
                                    last_mm = mm(ring[2 * u + o], WS[:, a, h, o * P:(o + 1) * P], parts[:, c, h, :],
                                                 start=(h == 0 and m == 0), stop=(h == NH - 1 and m == len(PARTS) - 1))
                                if h == NH - 1:
                                    last_mm.then_inc(ring_full, 1)
                                elif o == NH - 1:
                                    last_mm.then_inc(x1_used, 1)
                        if first and u == 0:
                            output_constants()

                final_pair(0, True)
                if last:
                    with pe.Fori(1, NPR) as i:
                        final_pair(i)
                    return
                with pe.Fori(1, NPR - 3) as i:
                    final_pair(i)
                b0_means(b + 1)
                final_pair(NPR - 3)
                b0_variances(b + 1)
                for i in range(NPR - 2, NPR):
                    final_pair(i)

            b0_means(0)
            b0_variances(0)
            with pe.Fori(0, B - 1) as b:
                image(b, False)
            image(B - 1, True)

        @block.vector
        def _(dve):
            v_ = nc.vector
            tr = 0
            for dst in (wqT[:, 0, :], wqT[:, 1, :], convT[:, 0:P], convT[:, P:C], w1T[:, 0, :], w1T[:, 1, :]):
                dve.wait_ge(w_tr, tr + 1)
                if tr < 2:
                    for t, c in ((0, 0), (1, 2), (2, 1)):
                        last = v_.tensor_copy(dst[:, c * HID:(c + 1) * HID], PS[:, tr % 2, t * P:(t + 1) * P])
                else:
                    last = v_.tensor_copy(dst, PS[:, tr % 2, 0:dst.shape[1]])
                last.then_inc(w_cp, 1)
                tr += 1
            dve.drain()
            for s, n in ((v_ready, 2), (q_shift, 1), (ring_used, 4), (cg_used, 2), (qv_ready, 2),
                         (ek_ready, 1), (eT_sb, 1), (qT_sb, 1), (alpha_ready, 1), (sq_done, 2)):
                dve.sem_inc(s, n)
            dve.wait_ge(consts, 1)

            def stats(b, i, u):
                dve.wait_ge(x_in[u], b * (NQ * 16) + i * 16 + 32)
                for k in range(2):
                    for h in range(NH):
                        v_.bn_stats(bn[:, h, bass.ds(i * 8 + (2 * u + k), 1), :].rearrange("p a s -> p (a s)"),
                                    x_sb[:, h, bass.ds(i * (8 * T) + (2 * u + k) * T, T)])

            def low(g, c, u, h):
                dve.wait_ge(xh_ready, 2 * g + (h + 1))
                ins = v_.scalar_tensor_tensor(xhl[:, u, 1, h, :], x_sb[:, h, bass.ds(c, T)], NM[:, h:h + 1],
                                              xhl[:, u, 0, h, :].bitcast(F32), ALU.add, ALU.subtract)
                if h == NH - 1:
                    ins.then_inc(xl_ready, 1)

            def maximum_k(g, u):
                dve.wait_ge(k_ready, g + 1)
                v_.tensor_reduce(negk[:, :], ps_k, axis=AXX, op=ALU.max, negate=True)
                dve.drain()
                dve.wait_ge(alpha_ready, g + 1)
                v_.tensor_tensor(negmax[:, u:u + 1], negmax[:, 1 - u:2 - u], negk[:, :], ALU.min)\
                    .then_inc(negmax_ready, 1)

            def maximum_q(g, u):
                dve.wait_ge(qv_ready, g + 3)
                q4 = ps_qv[u][:, :, 0:HID].rearrange("p t (e d) -> p t e d", d=DH)
                qm4 = qm[:, :].rearrange("p (t e) -> p t e", e=HEADS)
                v_.tensor_reduce(qm4, q4, axis=AXX, op=ALU.max)
                dve.drain()
                v_.tensor_tensor(q_sb[:, u, :, :].rearrange("p (t e) d -> p t e d", e=HEADS), q4,
                                 qm4[:, :, :, None].to_broadcast([P, NT, HEADS, DH]), ALU.subtract)\
                    .then_inc(q_shift, 1)

            def accumulate(g, u):
                dve.wait_ge(cg_ready, g + 3)
                dve.wait_ge(alpha_ready, g + 2)
                v_.scalar_tensor_tensor(acc[:, :], acc[:, :], alpha[:, u:u + 1], ps_cg[:, 2 * HID:2 * HID + G1],
                                        ALU.mult, ALU.add)
                v_.tensor_tensor(gram[:, :], gram[:, :], ps_cg[:, 0:2 * HID], ALU.add).then_inc(cg_used, 1)

            def sums(g, u):
                dve.wait_ge(q_exp, g + 1)
                v_.tensor_reduce(qsum[:, :], q_sb[:, u, :, :], axis=AXX, op=ALU.add)
                dve.drain()
                v_.reciprocal(qinv[:, u, :], qsum[:, :]).then_inc(q_inv, 1)


            def final(b, i, u, k):
                for h in range(NH):
                    dve.wait_ge(ring_full, b * RING + i * 16 + (2 * NCH + 4 * u + 2 * k + h + 1) + 5)
                    xc = x_sb[:, h, bass.ds(i * (8 * T) + (2 * u + k) * T, T)]
                    v_.scalar_tensor_tensor(xc, ring[2 * k + h], DD[:, h:h + 1], xc, ALU.add, ALU.add)\
                        .then_inc(ring_used, 1)

            def final_pair(b, i, u):
                for k in range(2):
                    final(b, i, u, k)

            def b0_aggregate(b):
                dve.drain()
                for h in range(NH):
                    ins = v_.bn_aggr(mv[:, h, :], bn[:, h, :, :].rearrange("p c s -> p (c s)"))
                ins.then_inc(xstat_ready, 1)
                dve.drain()
                v_.tensor_scalar(NB, mv[:, :, 0], -1.0, None, ALU.mult)

            def b0_means(b):
                dve.wait_ge(xmean_ps, b + 1)
                v_.tensor_scalar(NM, ps_cg[:, 0:NH], -1.0, None, ALU.mult).then_inc(nm_ready, 1)
                v_.tensor_tensor(DEV, mv[:, :, 0], ps_cg[:, 0:NH], ALU.subtract)
                dve.drain()
                v_.tensor_tensor(D2, DEV, DEV, ALU.mult)
                dve.drain()
                v_.tensor_tensor(SVAR, mv[:, :, 1], D2, ALU.add).then_inc(xvar_ready, 1)

            def b0_variances(b):
                dve.wait_ge(xgvar_ps, b + 1)
                v_.tensor_scalar(S1, ps_cg[:, 8:8 + NH], EPS, None, ALU.add).then_inc(xgvar_ready, 1)

            def b0_weights(b):
                dve.wait_ge(wh_ready, b + 1)
                for h in range(NH):
                    ins = v_.scalar_tensor_tensor(wqvk[:, 1, h, :], wqT[:, h, :], RR[:, h:h + 1],
                                                  wqvk[:, 0, h, :].bitcast(F32), ALU.mult, ALU.subtract)
                ins.then_inc(wl_ready, 1)

            def b0_low(b, u):
                for h in range(NH):
                    low(b * NCH + u, u * T, u, h)

            def image(b, last):
                c0 = b * NCH
                v_.memset(acc[:, :], 0.0)
                v_.memset(gram[:, :], 0.0)
                v_.memset(negmax[:, 1:2], BIG)
                maximum_k(c0, 0)

                def stage_stats(i, h):
                    dve.wait_ge(stage_in[h], b * (NPR * 16) + i * 16 + 16)
                    v_.bn_stats(bn[:, h, bass.ds(i + NPR, 1), :].rearrange("p a s -> p (a s)"), stage[:, h, :])\
                        .then_inc(stage_used, 1)

                def step(c, i, u, low_next=True, k_next=True, sum_last=True):
                    g = c0 + c
                    maximum_q(g, u)
                    if low_next:
                        low(g + 2, (c + 2) * T, u, 0)
                    if not k_next:
                        accumulate(g - 1, 1 - u)
                        sums(g, u)
                        return
                    sums(g, u)
                    maximum_k(g + 1, 1 - u)
                    if sum_last:
                        accumulate(g - 1, 1 - u)
                    if low_next:
                        low(g + 2, (c + 2) * T, u, 1)
                    if not last:
                        stage_stats(i, u)

                step(0, 0, 0, sum_last=False)
                with dve.Fori(0, NPR - 2) as i:
                    for u in range(2):
                        step(i * 2 + u + 1, i + u, 1 - u)
                step(NCH - 3, NPR - 2, 1)
                step(NCH - 2, NPR - 1, 0, low_next=False)
                step(NCH - 1, NPR - 1, 1, low_next=False, k_next=False)
                dve.drain()
                dve.wait_ge(ctx_end, b + 1)
                v_.scalar_tensor_tensor(acc[:, :], acc[:, :], alpha[:, 1:2], ps_cg[:, 2 * HID:2 * HID + G1],
                                        ALU.mult, ALU.add)
                dve.drain()
                v_.reciprocal(DEV[:, 0:1], acc[:, HID:G1])
                dve.drain()
                v_.scalar_tensor_tensor(ctxm[:, :], acc[:, 0:HID], DEV[:, 0:1], headmask[:, :], ALU.mult, ALU.mult)\
                    .then_inc(ctxm_ready, 1)
                if not last:
                    stage_stats(NPR - 1, 1)
                dve.wait_ge(cg_ready, c0 + NCH + 2)
                v_.tensor_tensor(gram[:, :], gram[:, :], ps_cg[:, 0:2 * HID], ALU.add).then_inc(cg_used, 1)
                dve.drain()
                v_.scalar_tensor_tensor(gram_q[:, :], gram[:, HID:2 * HID], 2.0, gram[:, 0:HID], ALU.mult, ALU.add)\
                    .then_inc(gram_ready, 1)
                dve.wait_ge(qT_sb, c0 + NCH + 1)
                v_.tensor_reduce(mu[:, 0:1], qs[:, :], axis=AXX, op=ALU.add)
                dve.drain()
                v_.tensor_scalar(mu[:, 1:2], mu[:, 0:1], 1.0 / N, None, ALU.mult).then_inc(mu_ready, 1)
                dve.wait_ge(w_in[3], 80)
                dve.wait_ge(gram_mt_ps, b + 1)
                v_.tensor_copy(DELTA, ps_qT[:, C:C + NH])
                v_.scalar_tensor_tensor(pz[:, :], ps_k[:, 0:C], 1.0 / N, MT[:, :], ALU.mult, ALU.mult)\
                    .then_inc(pz_ready, 1)
                dve.drain()
                v_.tensor_tensor(D2, DELTA, DELTA, ALU.mult)
                v_.tensor_tensor(TT, vecs[:, 0, :], DELTA, ALU.add)
                dve.drain()
                dve.wait_ge(yvar_ps, b + 1)
                v_.tensor_tensor(VAR1, ps_qT[:, C + 4:C + 4 + NH], D2, ALU.subtract)
                dve.drain()
                v_.tensor_scalar(VB, VAR1, 0.0, EPS, ALU.max, ALU.add).then_inc(yvar_ready, 1)
                v_.tensor_tensor(TT, vecs[:, 0, :], TT, ALU.subtract)
                dve.wait_ge(ydev_ready, b + 1)
                v_.tensor_tensor(A, RS, vecs[:, 1, :], ALU.mult)
                dve.drain()
                def mixed_pair(i):
                    for u in range(2):
                        for h in range(NH):
                            n = 2 * u + h
                            dve.wait_ge(ring_full, b * RING + i * 4 + n + 6)
                            xc = x_sb[:, h, bass.ds(i * (2 * T) + u * T, T)]
                            v_.scalar_tensor_tensor(xc, ring[n], A[:, h:h + 1], xc, ALU.mult, ALU.add)\
                                .then_inc(ring_used, 1)

                mixed_pair(0)
                v_.tensor_tensor(AD, A, DELTA, ALU.mult)
                v_.tensor_tensor(CC, TT, A, ALU.mult)
                dve.drain()
                v_.tensor_tensor(MEAN1, mv[:, :, 0], AD, ALU.add)
                v_.tensor_tensor(CC, CC, vecs[:, 2, :], ALU.add)
                dve.drain()
                v_.tensor_tensor(MEAN1, MEAN1, CC, ALU.add).then_inc(mean1_ready, 1)
                v_.tensor_tensor(D2, AD, AD, ALU.mult)
                with dve.Fori(1, NPR) as i:
                    mixed_pair(i)
                dve.drain()
                dve.wait_ge(gmean1_ps, b + 1)
                v_.tensor_tensor(DEV1, MEAN1, ps_cg[:, 0:NH], ALU.subtract)
                v_.tensor_tensor(VEC, CC, ps_cg[:, 0:NH], ALU.subtract)
                dve.drain()
                v_.tensor_tensor(DEV, DEV1, DEV1, ALU.mult)
                for h in range(NH):
                    v_.tensor_scalar(pooled[:, h, :], ones[:, :], DEV1[:, h:h + 1], None, ALU.mult)
                dve.drain()
                v_.tensor_tensor(D2, DEV, D2, ALU.subtract)
                dve.wait_ge(sq_done, (b + 1) * (2 * NCH) + 2)
                v_.tensor_reduce(SQS, sq[:, :, :], axis=AXX, op=ALU.add)
                dve.drain()
                v_.scalar_tensor_tensor(SVAR, SQS, 1.0 / N, D2, ALU.mult, ALU.add).then_inc(var1_ready, 1)
                dve.wait_ge(gvar1_ps, b + 1)
                v_.tensor_scalar(S1, ps_cg[:, 8:8 + NH], EPS, None, ALU.add).then_inc(gvar1_ready, 1)
                dve.wait_ge(dev1_ready, b + 1)
                for h in range(NH):
                    ins = v_.tensor_scalar(se1R[:, h, :], se1T[:, h, :], R1[:, h:h + 1], None, ALU.mult)
                ins.then_inc(se1r_ready, 1)
                v_.tensor_tensor(VEC, VEC, R1, ALU.mult)
                dve.wait_ge(hidden_exp, b + 1)
                v_.tensor_scalar(hid[:, 1, :], hid[:, 0, :], 1.0, None, ALU.add)
                dve.drain()
                v_.reciprocal(hid[:, 2, :], hid[:, 1, :])
                dve.drain()
                v_.tensor_tensor(hid[:, 3, :], ps_qT[:, 8:8 + J], hid[:, 2, :], ALU.mult).then_inc(hid_ready, 1)
                dve.drain()
                for n in range(2):
                    v_.tensor_scalar(diag[n], ident[:, :], hid[:, 3, JD + JP + n:JD + JP + n + 1], None, ALU.mult)\
                        .then_inc(diag_dve, 1)
                for h in range(NH):
                    dve.wait_ge(se_in[h], (b + 1) * 32)
                for j in range(JD):
                    for h in range(NH):
                        if j > 0:
                            dve.wait_ge(wb_step, b * (2 * JD) + 2 * j + h - 1)
                        v_.scalar_tensor_tensor(WB[:, h, :], se_sb[h].rearrange("p (o j) -> p o j", j=J)[:, :, j],
                                                hid[:, 3, j:j + 1], w1T[:, h, :] if j == 0 else WB[:, h, :],
                                                ALU.mult, ALU.add).then_inc(wb_step, 1)
                dve.drain()
                dve.wait_ge(prod_used, (b + 1) * (JP - 1))
                v_.tensor_tensor(WB[:, :, :].rearrange("p h o -> p (h o)"), WB[:, :, :].rearrange("p h o -> p (h o)"),
                                 wsum, ALU.add)
                dve.drain()
                dve.wait_ge(wb_ready, b + 1)
                for h in range(NH):
                    v_.tensor_tensor(WB[:, h, :], WB[:, h, :], ps_wb[h], ALU.add)
                dve.drain()
                for h in range(NH):
                    v_.tensor_scalar(WS[:, 0, h, :], WB[:, h, :], R1[:, h:h + 1], None, ALU.mult)
                dve.drain()
                for h in range(NH):
                    v_.scalar_tensor_tensor(WS[:, 1, h, :], WB[:, h, :], R1[:, h:h + 1],
                                            WS[:, 0, h, :].bitcast(F32), ALU.mult, ALU.subtract)\
                        .then_inc(ws_ready, 1)
                dve.wait_ge(const_ps, b + 1)
                v_.tensor_tensor(DD, CC, ps_cg[:, 16:16 + NH], ALU.add)
                dve.drain()
                if last:
                    with dve.Fori(0, NQ) as i:
                        for u in range(4):
                            final_pair(b, i, u)
                    return
                for u in range(4):
                    final_pair(b, 0, u)
                with dve.Fori(0, NQ // 2) as i:
                    for u in range(4):
                        final_pair(b, i + 1, u)
                        stats(b + 1, i, u)
                b0_aggregate(b + 1)
                final_pair(b, NQ - 1, 0)
                b0_means(b + 1)
                final_pair(b, NQ - 1, 1)
                b0_variances(b + 1)
                final_pair(b, NQ - 1, 2)
                b0_weights(b + 1)
                final(b, NQ - 1, 3, 0)
                b0_low(b + 1, 0)
                final(b, NQ - 1, 3, 1)
                b0_low(b + 1, 1)

            with dve.Fori(0, NQ) as i:
                for u in range(4):
                    stats(0, i, u)
            b0_aggregate(0)
            b0_means(0)
            b0_variances(0)
            b0_weights(0)
            for u in range(2):
                b0_low(0, u)
            with dve.Fori(0, B - 1) as b:
                image(b, False)
            image(B - 1, True)


_INS = ["x", "L0_conv_qkv_w", "L0_conv_conv_w", "L0_conv_conv_b", "L0_conv_gamma", "L0_conv_beta",
        "L1_conv_w_conv", "L1_conv_w_se1", "L1_conv_w_se_out"]


def kernel(**inputs):
    import numpy as _np
    import concourse.bacc as _bacc
    from concourse import mybir as _mybir
    from concourse.bass_utils import run_bass_kernel_spmd as _run

    nc = _bacc.Bacc("TRN2", target_bir_lowering=False, num_devices=1)
    arrays, args = {}, []
    for name in _INS:
        a = _np.ascontiguousarray(inputs[name])
        arrays[f"in_{name}"] = a
        args.append(nc.dram_tensor(f"in_{name}", a.shape, _mybir.dt.from_np(a.dtype), kind="ExternalInput").ap())
    shape = arrays["in_x"].shape
    args.append(nc.dram_tensor("out_x2", shape, _mybir.dt.float32, kind="ExternalOutput").ap())
    block_program(nc, *args)
    r = _run(nc, [arrays], core_ids=[0])
    return r.results[0]["out_x2"]
```
